# Optimizing a Trainium2 kernel written in Bass

```python
import numpy as np
import jax
import jax.numpy as jnp

def _softmax(x, axis=-1):
    return jax.nn.softmax(x, axis=axis)

def _gelu(x):
    return jax.nn.gelu(x, approximate=True)

def _silu(x):
    return jax.nn.silu(x)

def _sigmoid(x):
    return jax.nn.sigmoid(x)

def _layernorm(x, axis=-1, eps=1e-05):
    m = jnp.mean(x, axis=axis, keepdims=True)
    v = jnp.var(x, axis=axis, keepdims=True)
    return (x - m) / jnp.sqrt(v + eps)

def _scatter_add(tgt, idx, src, axis=0):
    return tgt.at[idx].add(src)

def _segment_sum(src, seg, n):
    return jax.ops.segment_sum(src, seg, n)
kernel_name = 'mk_lm_tower_d1_tok_ids1024_r4_59b096'

def setup_inputs(seed: int=0):
    np.random.seed(seed)
    _w = jnp.asarray

    def _rec_inputs():
        import jax
        import jax.numpy as jnp
        _rk = jax.random.key(seed)
        x = jax.random.randint(jax.random.fold_in(_rk, 1), (16, 256), 0, 12564, jnp.int32)
        return x
    x = _rec_inputs()

    def _L0_tok_setup():
        import jax, jax.numpy as jnp
        import numpy as np
        VOCAB = 50257
        D_MODEL = 256
        BATCH = 4
        SEQ = 1024
        key = jax.random.key(seed)
        k_ids, k_w = jax.random.split(key)
        input = jax.random.randint(k_ids, (BATCH, SEQ), 0, VOCAB, dtype=jnp.int32)
        W = jax.random.normal(k_w, (D_MODEL, VOCAB), dtype=jnp.float32) * (1.0 / np.sqrt(VOCAB))
        return {'input': input, 'W': W}
    _L0_tok_all = _L0_tok_setup()
    _L0_tok_in = {k: v for k, v in _L0_tok_all.items() if k in ('W',)}
    del _L0_tok_all

    def _L0_attn_setup():
        import jax, jax.numpy as jnp
        import numpy as np
        DIM = 256
        DEPTH = 6
        LN_EPS = 1e-05

        def _layernorm(x, gamma, beta):
            mu = jnp.mean(x, axis=-1, keepdims=True)
            var = jnp.mean(jnp.square(x - mu), axis=-1, keepdims=True)
            return (x - mu) * jax.lax.rsqrt(var + LN_EPS) * gamma + beta
        key = jax.random.key(seed)
        ks = jax.random.split(key, 6)
        b, n, d = (4, 512, DIM)
        x = jax.random.normal(ks[0], (b, n, d), dtype=jnp.float32)
        w_qkv = jax.random.normal(ks[1], (DEPTH, d, 3 * d), dtype=jnp.float32) * 0.02
        w_out = jax.random.normal(ks[2], (DEPTH, d, d), dtype=jnp.float32) * 0.02
        b_out = jnp.zeros((DEPTH, d), dtype=jnp.float32)
        gamma = jnp.ones((DEPTH, d), dtype=jnp.float32)
        beta = jnp.zeros((DEPTH, d), dtype=jnp.float32)
        return {'x': x, 'w_qkv': w_qkv, 'w_out': w_out, 'b_out': b_out, 'gamma': gamma, 'beta': beta}
    _L0_attn_all = _L0_attn_setup()
    _L0_attn_in = {k: v for k, v in _L0_attn_all.items() if k in ('w_qkv', 'w_out', 'b_out', 'gamma', 'beta')}
    del _L0_attn_all

    def _L0_ffn_setup():
        import jax, jax.numpy as jnp
        import numpy as np
        EXPERTS = 8
        TOP_K = 2

        def swiglu(x, w1, w2, w3):
            h = x @ w1
            return h * jax.nn.sigmoid(h) * (x @ w2) @ w3
        key = jax.random.key(seed)
        ks = jax.random.split(key, 9)
        B, S, D = (4, 512, 256)
        H = 2 * D
        s = 0.02
        x = jax.random.normal(ks[0], (B, S, D), dtype=jnp.float32)
        gate_w = jax.random.normal(ks[1], (D, EXPERTS), dtype=jnp.float32) * s
        ew1 = jax.random.normal(ks[2], (EXPERTS, D, H), dtype=jnp.float32) * s
        ew2 = jax.random.normal(ks[3], (EXPERTS, D, H), dtype=jnp.float32) * s
        ew3 = jax.random.normal(ks[4], (EXPERTS, H, D), dtype=jnp.float32) * s
        sw1 = jax.random.normal(ks[5], (D, H), dtype=jnp.float32) * s
        sw2 = jax.random.normal(ks[6], (D, H), dtype=jnp.float32) * s
        sw3 = jax.random.normal(ks[7], (H, D), dtype=jnp.float32) * s
        return {'x': x, 'gate_w': gate_w, 'ew1': ew1, 'ew2': ew2, 'ew3': ew3, 'sw1': sw1, 'sw2': sw2, 'sw3': sw3}
    _L0_ffn_all = _L0_ffn_setup()
    _L0_ffn_in = {k: v for k, v in _L0_ffn_all.items() if k in ('gate_w', 'ew1', 'ew2', 'ew3', 'sw1', 'sw2', 'sw3')}
    del _L0_ffn_all
    return {'x': x, 'L0_tok_W': _L0_tok_in['W'], 'L0_attn_w_qkv': _L0_attn_in['w_qkv'], 'L0_attn_w_out': _L0_attn_in['w_out'], 'L0_attn_b_out': _L0_attn_in['b_out'], 'L0_attn_gamma': _L0_attn_in['gamma'], 'L0_attn_beta': _L0_attn_in['beta'], 'L0_ffn_gate_w': _L0_ffn_in['gate_w'], 'L0_ffn_ew1': _L0_ffn_in['ew1'], 'L0_ffn_ew2': _L0_ffn_in['ew2'], 'L0_ffn_ew3': _L0_ffn_in['ew3'], 'L0_ffn_sw1': _L0_ffn_in['sw1'], 'L0_ffn_sw2': _L0_ffn_in['sw2'], 'L0_ffn_sw3': _L0_ffn_in['sw3']}

def reference(x, L0_tok_W, L0_attn_w_qkv, L0_attn_w_out, L0_attn_b_out, L0_attn_gamma, L0_attn_beta, L0_ffn_gate_w, L0_ffn_ew1, L0_ffn_ew2, L0_ffn_ew3, L0_ffn_sw1, L0_ffn_sw2, L0_ffn_sw3):
    import jax
    import jax.numpy as jnp

    def _L0_tok_ref(input, W):
        import jax, jax.numpy as jnp
        import numpy as np
        VOCAB = 50257
        D_MODEL = 256
        BATCH = 4
        SEQ = 1024
        return jnp.take(W.T, input, axis=0)

    def _L0_attn_ref(x, w_qkv, w_out, b_out, gamma, beta):
        import jax, jax.numpy as jnp
        import numpy as np
        DIM = 256
        DEPTH = 6
        LN_EPS = 1e-05

        def _layernorm(x, gamma, beta):
            mu = jnp.mean(x, axis=-1, keepdims=True)
            var = jnp.mean(jnp.square(x - mu), axis=-1, keepdims=True)
            return (x - mu) * jax.lax.rsqrt(var + LN_EPS) * gamma + beta
        depth = w_qkv.shape[0]
        for l in range(depth):
            residual = x
            h = _layernorm(x, gamma[l], beta[l])
            qkv = h @ w_qkv[l]
            q, k, v = jnp.split(qkv, 3, axis=-1)
            q = jax.nn.softmax(q, axis=1)
            k = jax.nn.softmax(k, axis=2)
            context = jnp.einsum('bic,bjc->bij', k, v)
            out = jnp.einsum('bic,bij->bjc', q, context)
            out = out @ w_out[l] + b_out[l]
            x = out + residual
        return x

    def _L0_ffn_ref(x, gate_w, ew1, ew2, ew3, sw1, sw2, sw3):
        import jax, jax.numpy as jnp
        import numpy as np
        EXPERTS = 8
        TOP_K = 2

        def swiglu(x, w1, w2, w3):
            h = x @ w1
            return h * jax.nn.sigmoid(h) * (x @ w2) @ w3
        B, S, D = x.shape
        gate_out = x @ gate_w
        top_v, top_i = jax.lax.top_k(gate_out, TOP_K)
        masked = jnp.full_like(gate_out, -1e+20)
        bi = jnp.arange(B)[:, None, None]
        si = jnp.arange(S)[None, :, None]
        masked = masked.at[bi, si, top_i].set(top_v)
        probs = jax.nn.softmax(masked, axis=-1)
        chosen = jnp.zeros_like(gate_out, dtype=bool).at[bi, si, top_i].set(True)
        w = jnp.where(chosen, probs, 0.0)

        def one_expert(w1, w2, w3, we):
            return swiglu(x, w1, w2, w3) * we[..., None]
        out = jax.vmap(one_expert, in_axes=(0, 0, 0, 2))(ew1, ew2, ew3, w).sum(0)
        out = out + swiglu(x, sw1, sw2, sw3)
        return out
    h = _L0_tok_ref(x, L0_tok_W)
    h = h + _L0_attn_ref(_layernorm(h, axis=-1), L0_attn_w_qkv, L0_attn_w_out, L0_attn_b_out, L0_attn_gamma, L0_attn_beta)
    h = h + _L0_ffn_ref(_layernorm(h, axis=-1), L0_ffn_gate_w, L0_ffn_ew1, L0_ffn_ew2, L0_ffn_ew3, L0_ffn_sw1, L0_ffn_sw2, L0_ffn_sw3)
    return h

_drawn_inputs = setup_inputs


def setup_inputs(seed=0):
    import zlib

    import numpy as np

    out = dict(_drawn_inputs(seed))
    spreads = {'L0_attn_b_out': (0.0, 0.1), 'L0_attn_gamma': (1.0, 0.6), 'L0_attn_beta': (0.0, 0.8)}
    factors = {'L0_attn_w_qkv': 3.045,
     'L0_attn_w_out': 2.896,
     'L0_ffn_gate_w': 3.305,
     'L0_ffn_ew1': 2.868,
     'L0_ffn_ew2': 2.837,
     'L0_ffn_ew3': 2.83}
    for name, (base, spread) in spreads.items():
        noise = np.random.default_rng([zlib.crc32(name.encode()), seed]).standard_normal(out[name].shape)
        drawn = base * np.exp(spread * noise) if base else spread * noise
        out[name] = jnp.asarray(drawn.astype(out[name].dtype))
    for name, factor in factors.items():
        out[name] = (out[name] * factor).astype(out[name].dtype)
    return out
```

```python
from contextlib import ExitStack

import numpy as np

import concourse.bass as bass
from concourse import mybir

P = 128


def tower(nc, x_ids, tok_w, w_qkv, w_out, b_out, gamma, beta, gate_w, ew1, ew2, ew3, sw1, sw2, sw3, out):
    f32, f16, i32 = mybir.dt.float32, mybir.dt.float16, mybir.dt.int32
    ALU = mybir.AluOpType
    ACT = mybir.ActivationFunctionType
    AX = mybir.AxisListType

    NB, SEQ = x_ids.shape
    D, VOCAB = tok_w.shape
    DEPTH = w_qkv.shape[0]
    E, _, HID = ew1.shape
    TOK = NB * SEQ
    NT = TOK // P
    TB = SEQ // P
    KH = D // P
    HC = HID // P
    NE = E + 1
    ITEMS = DEPTH * NB
    EPS = 1e-5
    WS = 64.0
    KS = 4096.0
    PS = 256.0

    VCH = 512
    VBUF = 4
    VSTEP = VCH * VBUF
    VBLK = VCH // P
    STRETCH = 7
    VROWS = STRETCH * VSTEP
    NSTRETCH = -(-VOCAB // VROWS)

    def first_column(eng, step, j):
        v, last = step * VSTEP + j * VCH, VOCAB - VCH
        return eng.snap(v - (v > last) * (v - last)).with_bounds(min_val=0, max_val=last, guaranteed_mod_val=0, out_of_modulus=1)

    emb_rows = nc.dram_tensor("emb_rows", (VROWS, D), f32, kind="Internal").ap()
    h0_rows = nc.dram_tensor("h0_rows", (TOK, D), f32, kind="Internal").ap()

    def wait(eng, sem, value):
        if not (isinstance(value, int) and value <= 0):
            eng.wait_ge(sem, value)

    ctx = ExitStack()
    with ctx:
        def sb(name, shape, dt, where=ctx):
            return where.enter_context(nc.sbuf_tensor(name, shape, dt))

        def sem(name):
            return ctx.enter_context(nc.semaphore(name))

        X = sb("X", [P, NT, D], f32)
        W12h = sb("W12h", [P, NE, KH, 2 * HID], f16)
        W12l = sb("W12l", [P, NE, KH, 2 * HID], f16)
        W3h = sb("W3h", [P, NE, HC, D], f16)
        W3l = sb("W3l", [P, NE, HC, D], f16)
        ident = sb("ident", [P, P], f32)
        ident16 = sb("ident16", [P, P], f16)
        idx = sb("idx", [P, NT], i32)
        epst = sb("epst", [P, TB], f32)
        mhalf = sb("mhalf", [P, NT], f32)
        stats = sb("stats", [P, 8, 6], f32)
        mv = sb("mv", [P, NT, 2], f32)
        rstd = sb("rstd", [P, NT], f32)
        h0b = sb("h0b", [P, 2, 4, D], f32)

        pb = [ctx.enter_context(nc.psum_tensor(f"bank{i}", [P, 512], f32)) for i in range(8)]

        s_ids = sem("s_ids")
        s_idrow = sem("s_idrow")
        s_const = sem("s_const")
        s_wload = [sem(f"s_wload{i}") for i in range(VBUF)]
        s_wtr = [sem(f"s_wtr{i}") for i in range(VBUF)]
        s_wcp = [sem(f"s_wcp{i}") for i in range(VBUF)]
        s_wst = [sem(f"s_wst{i}") for i in range(VBUF)]
        s_fstage = [sem(f"s_fstage{i}") for i in range(2)]
        s_fhi, s_flo = sem("s_fhi"), sem("s_flo")
        s_gath = [sem(f"s_gath{i}") for i in range(4)]
        s_h0st = [sem(f"s_h0st{i}") for i in range(4)]
        s_reuse, s_passed = sem("s_reuse"), sem("s_passed")
        s_id, s_idmax, s_wstage, s_gap = sem("s_id"), sem("s_idmax"), sem("s_wstage"), sem("s_gap")
        s_st, s_stat, s_var, s_rstd, s_norm = sem("s_st"), sem("s_stat"), sem("s_var"), sem("s_rstd"), sem("s_norm")

        NG4 = NT // 4
        emb = ExitStack()
        VW = [sb(f"VW{i}", [P, KH, VCH], f32, emb) for i in range(VBUF)]
        VR = [sb(f"VR{i}", [P, VBLK, D], f32, emb) for i in range(VBUF)]
        FST = [sb(f"FST{i}", [P, KH * 2 * HID + HC * D], f32, emb) for i in range(2)]
        idrow = W3l[0:1, :, :, :].rearrange("p e c n -> p (e c n)").bitcast(i32)[:, 0:TOK]
        idmax = sb("idmax", [1, 1], i32, emb)
        emb.close()

        FW12 = KH * 2 * HID

        att = ExitStack()
        WQKV = KH * 3 * D
        WL = WQKV + KH * D
        Wst = sb("Wst", [P, WL], f32, att)
        WSL = NB // 2
        WSN = WL // WSL
        Wsc = sb("Wsc", [P, WSN], f32, att)
        Wn = sb("Wn", [P, 2, WL], f16, att)
        Wc = sb("Wc", [P, 2, WL], f16, att)
        rows = sb("rows", [P, 2, 3, D], f32, att)
        xn = sb("xn", [P, TB, D], f32, att)
        amv = sb("amv", [P, TB, 2], f32, att)
        avar, arstd = sb("avar", [P, TB], f32, att), sb("arstd", [P, TB], f32, att)
        hf = sb("hf", [P, TB, D], f32, att)
        hhl = sb("hhl", [P, 2, TB, D], f16, att)
        hT = sb("hT", [P, 2, KH, SEQ], f16, att)
        EQ = sb("EQ", [P, KH, SEQ], f32, att)
        EQhl = sb("EQhl", [P, 2, KH, SEQ], f16, att)
        eqT = sb("eqT", [P, 2, TB, D], f16, att)
        EK = sb("EK", [P, TB, D], f32, att)
        khl = sb("khl", [P, 2, TB, D], f16, att)
        vT = sb("vT", [P, 2, KH, SEQ], f16, att)
        MT = sb("MT", [P, 2, KH, D], f16, att)
        PR = sb("PR", [P, 2, KH, D], f16, att)
        qmax, nqmax, zq, rzq = (sb(n, [P, KH], f32, att) for n in ("qmax", "nqmax", "zq", "rzq"))
        kmax, nkmax, zk, rzk, rzks = (sb(n, [P, TB], f32, att) for n in ("kmax", "nkmax", "zk", "rzk", "rzks"))
        att.close()

        s_rows = sem("s_rows")
        s_wsc, s_wnhi, s_wnlo = sem("s_wsc"), sem("s_wnhi"), sem("s_wnlo")
        s_wq, s_wk, s_wv, s_wo = sem("s_wq"), sem("s_wk"), sem("s_wv"), sem("s_wo")
        s_astat, s_amv, s_avar, s_arstd, s_xn = (sem(n) for n in ("s_astat", "s_amv", "s_avar", "s_arstd", "s_xn"))
        s_hg, s_hb, s_hhi, s_h, s_xb = (sem(n) for n in ("s_hg", "s_hb", "s_hhi", "s_h", "s_xb"))
        s_th, s_hT = sem("s_th"), sem("s_hT")
        s_q, s_qmax, s_nqmax, s_eq, s_eqhi, s_eqlo, s_tq, s_eqT, s_rzq = (
            sem(n) for n in ("s_q", "s_qmax", "s_nqmax", "s_eq", "s_eqhi", "s_eqlo", "s_tq", "s_eqT", "s_rzq"))
        s_k, s_kmax, s_nkmax, s_ek, s_rzk, s_rzks, s_khi, s_klo = (
            sem(n) for n in ("s_k", "s_kmax", "s_nkmax", "s_ek", "s_rzk", "s_rzks", "s_khi", "s_klo"))
        s_v, s_vhi, s_vlo = sem("s_v"), sem("s_vhi"), sem("s_vlo")
        s_m, s_mhi, s_mlo = sem("s_m"), sem("s_mhi"), sem("s_mlo")
        s_p, s_phi, s_plo = sem("s_p"), sem("s_phi"), sem("s_plo")
        s_o, s_x = sem("s_o"), sem("s_x")

        b_h, b_q, b_k, b_v, b_e, b_m, b_p, b_o = pb
        hT_ps = b_h[:, :].bitcast(f16).rearrange("p (a k n) -> p a k n", a=2, k=KH)
        eqT_ps = b_e[:, :].bitcast(f16).rearrange("p (a k n) -> p a k n", a=2, k=TB)
        q_ps = b_q[:, :].rearrange("p (k n) -> p k n", k=KH)
        k_ps = b_k[:, :].rearrange("p (k n) -> p k n", k=TB)
        v_ps = b_v[:, :].rearrange("p (k n) -> p k n", k=KH)
        m_ps = b_m[:, :].rearrange("p (k n) -> p k n", k=KH)
        p_ps = b_p[:, :].rearrange("p (k n) -> p k n", k=KH)
        o_ps = b_o[:, :].rearrange("p (k n) -> p k n", k=TB)

        ffn = ExitStack()
        xT = sb("xT", [P, 2, KH, TOK], f16, ffn)
        gw = sb("gw", [P, KH, E], f32, ffn)
        gates = sb("gates", [P, NT, E], f32, ffn)
        top8 = sb("top8", [P, NT, 8], f32, ffn)
        idx8 = sb("idx8", [P, NT, 8], mybir.dt.uint32, ffn)
        idxf = sb("idxf", [P, NT, 8], f32, ffn)
        iota8 = sb("iota8", [P, E], i32, ffn)
        iota8f = sb("iota8f", [P, E], f32, ffn)
        gap, gexp, gden = (sb(n, [P, NT], f32, ffn) for n in ("gap", "gexp", "gden"))
        prob = sb("prob", [P, 2, NT], f32, ffn)
        hot = sb("hot", [P, 2, NT, E], f32, ffn)
        wexp = sb("wexp", [P, NT, NE], f32, ffn)
        pre = ExitStack()
        xf = sb("xf", [P, 2, 4, D], f32, pre)
        xT32 = sb("xT32", [P, 2, KH, 4 * P], f32, pre)
        pre.close()
        silu = sb("silu", [P, 2, HC, P], f32, ffn)
        gT32 = sb("gT32", [P, 2, HC, P], f32, ffn)
        gThl = sb("gThl", [P, 2, 2, HC, P], f16, ffn)
        ffn.close()
        s_fst, s_fmv, s_fvar, s_frstd, s_xf = (sem(n) for n in ("s_fst", "s_fmv", "s_fvar", "s_frstd", "s_xf"))
        s_xfT, s_xThi, s_xT32, s_xTlo, s_gw, s_gate, s_gcp = (
            sem(n) for n in ("s_xfT", "s_xThi", "s_xT32", "s_xTlo", "s_gw", "s_gate", "s_gcp"))
        s_route = sem("s_route")
        s_gexp, s_iota = sem("s_gexp"), sem("s_iota")
        s_h12, s_silu, s_g, s_ghi, s_glo, s_y, s_acc = (
            sem(n) for n in ("s_h12", "s_silu", "s_g", "s_ghi", "s_glo", "s_y", "s_acc"))
        s_h0ld = [sem(f"s_h0ld{i}") for i in range(4)]
        s_h1 = sem("s_h1")
        s_out = sem("s_out")


        block = ctx.enter_context(nc.Block())

        def stretches(eng):
            eng.wait_ge(s_idmax, 1)
            return eng.snap(eng.value_load(idmax[0:1, 0:1], min_val=0, max_val=VOCAB - 1) // VROWS + 1)

        def steps(eng):
            return eng.snap(stretches(eng) * STRETCH)

        def layer(u):
            return u // NB

        def seq(u):
            return u % NB

        def tiles(u):
            return X[:, bass.ds(seq(u) * TB, TB), :]

        def wview(w, part, j, k, c0, n):
            at = k * 3 * D + j * D + c0 if j < 3 else WQKV + k * D + c0
            return w[:, part, at:at + n]

        PARTS = [(0, 0), (0, 1), (1, 0)]

        def item_loop(eng, one, lead, prepare=False):
            for t in range(-lead, 1):
                one(t, prepare and t == 0)
            if not prepare:
                with eng.Fori(1, ITEMS - lead) as t:
                    one(t, False)
            else:
                with eng.Fori(1, NB // 2) as t:
                    one(t, True)
                with eng.Fori(NB // 2, NB) as t:
                    one(t, False)
                with eng.Fori(1, DEPTH - 1) as l:
                    with eng.Fori(0, NB // 2) as b:
                        one(eng.snap(l * NB + b), True)
                    with eng.Fori(NB // 2, NB) as b:
                        one(eng.snap(l * NB + b), False)
                with eng.Fori(ITEMS - NB, ITEMS - lead) as t:
                    one(t, False)
            for t in range(ITEMS - lead, ITEMS):
                one(t, False)

        def have(u):
            return not isinstance(u, int) or 0 <= u < ITEMS

        @block.sync
        def _(sp):
            sp.dma_start(idrow[:, :], x_ids.rearrange("b s -> (b s)").rearrange("(a n) -> a n", a=1)).then_inc(s_idrow, 16)
            with nc.allow_non_contiguous_dma(reason="16 KB of token ids"):
                sp.dma_start(idx[:, :], x_ids.rearrange("b (t p) -> p (b t)", p=P)).then_inc(s_ids, 16)
            for e in range(NE):
                if e >= 2:
                    sp.wait_ge(s_flo, e - 1)
                w1, w2, w3 = (ew1[e], ew2[e], ew3[e]) if e < E else (sw1, sw2, sw3)
                st = FST[e % 2]
                st12 = st[:, 0:FW12].rearrange("p (k w n) -> p k w n", k=KH, w=2)
                sp.dma_start(st12[:, :, 0, :], w1.rearrange("(k p) n -> p k n", p=P)).then_inc(s_fstage[e % 2], 16)
                sp.dma_start(st12[:, :, 1, :], w2.rearrange("(k p) n -> p k n", p=P)).then_inc(s_fstage[e % 2], 16)
                sp.dma_start(st[:, FW12:].rearrange("p (c n) -> p c n", c=HC),
                             w3.rearrange("(c p) n -> p c n", p=P)).then_inc(s_fstage[e % 2], 16)
            src = tok_w.rearrange("(k p) v -> p k v", p=P)

            def load(step, v0, j):
                if not isinstance(step, int):
                    sp.wait_ge(s_wtr[j], step)
                sp.dma_start(VW[j][:, :, :], src[:, :, bass.ds(v0, VCH)]).then_inc(s_wload[j], 16)

            for j in range(VBUF):
                load(0, j * VCH, j)
            n = steps(sp)
            with sp.Fori(1, n) as step:
                for j in range(VBUF):
                    load(step, first_column(sp, step, j), j)
            for g in range(4):
                sp.wait_ge(s_gath[g], (n // STRETCH) * (16 * NT // 4))
                sp.dma_start(h0_rows.rearrange("(t p) d -> p t d", p=P)[:, g * NT // 4:(g + 1) * NT // 4, :],
                             X[:, g * NT // 4:(g + 1) * NT // 4, :]).then_inc(s_h0st[g], 16)
            sp.wait_ge(s_x, 1)
            for l in range(DEPTH):
                if l:
                    sp.wait_ge(s_wsc, WSL * l)
                sp.dma_start(Wst[:, 0:WQKV].rearrange("p (k n) -> p k n", k=KH),
                             w_qkv[l].rearrange("(k p) n -> p k n", p=P)).then_inc(s_wstage, 16)
                sp.dma_start(Wst[:, WQKV:].rearrange("p (k n) -> p k n", k=KH),
                             w_out[l].rearrange("(k p) n -> p k n", p=P)).then_inc(s_wstage, 16)
                if l:
                    sp.wait_ge(s_xb, NB * (l - 1) + 1)
                for r, v in enumerate((gamma, beta, b_out)):
                    sp.dma_start(rows[:, l % 2, r, :], v[l:l + 1, :].broadcast_to([P, D])).then_inc(s_rows, 16)
                sp.wait_ge(s_wnlo, WSL * (l + 1))
                for j, (used, ready) in enumerate(((s_q, s_wq), (s_k, s_wk), (s_v, s_wv), (s_p, s_wo))):
                    if l:
                        sp.wait_ge(used, NB * l)
                    if j < 3:
                        part = lambda w, a: w[:, a, 0:WQKV].rearrange("p (k j n) -> p k j n", k=KH, j=3)[:, :, j, :]
                    else:
                        part = lambda w, a: w[:, a, WQKV:]
                    for a in range(2):
                        sp.dma_start(part(Wc, a), part(Wn, a)).then_inc(ready, 16)
            for g in range(NG4):
                if g >= 2:
                    sp.wait_ge(s_h1, g - 1)
                else:
                    sp.wait_ge(s_h0st[3], 16)
                sp.dma_start(h0b[:, g % 2, :, :], h0_rows.rearrange("(t p) d -> p t d", p=P)[:, 4 * g:4 * g + 4, :])\
                  .then_inc(s_h0ld[g % 2], 16)
                if g == 1:
                    sp.wait_ge(s_x, NB + ITEMS)
                    sp.dma_start(gw[:, :, :], gate_w.rearrange("(k p) e -> p k e", p=P)).then_inc(s_gw, 16)
            for b in range(NB):
                sp.wait_ge(s_acc, (NE - 1) * NT + TB * (b + 1))
                sp.dma_start(out[b].rearrange("(t p) d -> p t d", p=P), X[:, TB * b:TB * b + TB, :]).then_inc(s_out, 16)
            sp.wait_ge(s_out, 16 * NB)

        @block.gpsimd
        def _(pool):
            pool.memset(ident[:, :], 0.0).then_inc(s_id, 1)
            pool.memset(mhalf[:, :], -0.5)
            pool.wait_ge(s_id, 1)
            pool.affine_select(out=ident[:, :], in_=ident[:, :], compare_op=ALU.not_equal, fill=1.0, base=0,
                               pattern=[[-1, P]], channel_multiplier=1).then_inc(s_id, 1)
            pool.wait_ge(s_id, 2)
            pool.tensor_copy(ident16[:, :], ident[:, :]).then_inc(s_const, 1)
            pool.memset(epst[:, :], EPS)
            pool.wait_ge(s_ids, 16)
            pool.sem_inc(s_reuse, 1)
            with pool.Fori(0, stretches(pool)) as q:
                for j in range(VBUF):
                    pool.wait_ge(s_wst[j], (q + 1) * (STRETCH * 16))
                pool.sem_inc(s_passed, 1)
                for t in range(NT):
                    pool.indirect_dma_start(out=X[:, t, :], out_offset=None, in_=emb_rows,
                                            in_offset=bass.IndirectOffsetOnAxis(ap=idx[:, t:t + 1], axis=0),
                                            bounds_check=VROWS - 1, oob_is_err=False)\
                        .then_inc(s_gath[t // 8], 16)
                for g in range(4):
                    pool.wait_ge(s_gath[g], (q + 1) * 128)
                pool.sem_inc(s_passed, 1)
                pool.tensor_scalar(idx[:, :], idx[:, :], -VROWS, None, ALU.add).then_inc(s_reuse, 1)
                pool.wait_ge(s_reuse, q + 2)
                pool.sem_inc(s_passed, 1)

            for g in range(4):
                pool.wait_ge(s_stat, 8 * (g + 1))
                v = mv[:, 8 * g:8 * g + 8, 1]
                pool.tensor_scalar(v, v, EPS, None, ALU.add).then_inc(s_var, 1)
                pool.wait_ge(s_var, g + 1)
                pool.tensor_tensor(rstd[:, 8 * g:8 * g + 8], v, mhalf[:, 0:8], ALU.pow).then_inc(s_rstd, 1)

            def cut(n):
                lo = bass.ds((n % WSL) * WSN, WSN)
                pool.wait_ge(s_wnhi, n + 1)
                pool.sem_inc(s_passed, 1)
                pool.tensor_tensor(Wn[:, 1, lo], Wsc[:, :], Wn[:, 0, lo], ALU.subtract).then_inc(s_wnlo, 1)

            for n in range(WSL):
                cut(n)

            def one(t, prep):
                u = t + 3
                if have(u):
                    pool.wait_ge(s_amv, u + 1)
                    pool.tensor_tensor(avar[:, :], amv[:, :, 1], epst[:, :], ALU.add).then_inc(s_avar, 1)
                    pool.wait_ge(s_avar, u + 1)
                    wait(pool, s_xn, u)
                    pool.tensor_tensor(arstd[:, :], avar[:, :], mhalf[:, 0:TB], ALU.pow).then_inc(s_arstd, 1)
                    pool.wait_ge(s_rows, 48 * (layer(u) + 1))
                    pool.wait_ge(s_xn, u + 1)
                    pool.sem_inc(s_passed, 1)
                    row = lambda r: rows[:, bass.ds(layer(u) % 2, 1), r, :].broadcast_to([P, TB, D])
                    pool.tensor_tensor(xn[:, :, :], xn[:, :, :], row(0), ALU.mult).then_inc(s_hg, 1)
                    pool.wait_ge(s_hg, u + 1)
                    wait(pool, s_th, u)
                    pool.sem_inc(s_passed, 1)
                    pool.tensor_tensor(hf[:, :, :], xn[:, :, :], row(1), ALU.add)
                    pool.tensor_tensor(hhl[:, 0, :, :], xn[:, :, :], row(1), ALU.add).then_inc(s_hhi, 1)
                    pool.wait_ge(s_hhi, u + 1)
                    pool.tensor_tensor(hhl[:, 1, :, :], hf[:, :, :], hhl[:, 0, :, :], ALU.subtract).then_inc(s_h, 1)
                    pool.tensor_tensor(tiles(u), tiles(u), row(2), ALU.add).then_inc(s_xb, 1)
                if prep:
                    cut(t + WSL if isinstance(t, int) else pool.snap(WSL * (layer(t) + 1) + t % WSL))

            item_loop(pool, one, 3, prepare=True)
            pool.wait_ge(s_x, NB + ITEMS)
            pool.iota(iota8[:, :], pattern=[[1, E]], base=0, channel_multiplier=0).then_inc(s_iota, 1)
            for g in range(NG4):
                pool.wait_ge(s_stat, NT + 4 * (g + 1))
                v = mv[:, 4 * g:4 * g + 4, 1]
                pool.tensor_scalar(v, v, EPS, None, ALU.add).then_inc(s_var, 1)
                pool.wait_ge(s_var, 4 + g + 1)
                pool.tensor_tensor(rstd[:, 4 * g:4 * g + 4], v, mhalf[:, 0:4], ALU.pow).then_inc(s_rstd, 1)

        @block.tensor
        def _(pe):
            mm = nc.tensor.matmul
            pe.wait_ge(s_const, 1)
            n = steps(pe)

            def chunk(step, j):
                pe.wait_ge(s_wload[j], (step + 1) * 16)
                if not (isinstance(step, int) and step == 0):
                    pe.wait_ge(s_wcp[j], step * 2)
                for v in range(VBLK):
                    for k in range(KH):
                        last = nc.tensor.transpose(pb[2 * j + v // 2][:, (v % 2) * D + k * P:(v % 2) * D + k * P + P],
                                                   VW[j][:, k, v * P:(v + 1) * P], ident[:, :])
                last.then_inc(s_wtr[j], 1)

            for j in range(VBUF):
                chunk(0, j)
            with pe.Fori(1, n) as step:
                for j in range(VBUF):
                    chunk(step, j)
            for j in range(VBUF):
                pe.wait_ge(s_wcp[j], n * 2)

            def product(dst, m, lhs, rhs, sem_):
                for o in range(m):
                    last = None
                    for i, (a, b) in enumerate(PARTS):
                        for k in range(2):
                            last = mm(dst[:, o, :], lhs(a, k, o), rhs(b, k), start=(i == 0 and k == 0), stop=(i == 2 and k == 1))
                last.then_inc(sem_, 1)

            def flip(dst, src, sem_):
                for a in range(2):
                    for k in range(2):
                        for t in range(2):
                            last = nc.tensor.transpose(dst[:, a, k, t * P:(t + 1) * P], src[:, a, t, k * P:(k + 1) * P], ident16[:, :])
                last.then_inc(sem_, 1)

            blk = lambda o: slice(o * P, (o + 1) * P)

            def one(t, prep):
                u = t + 1
                if have(u):
                    pe.wait_ge(s_hT, u + 1)
                    pe.wait_ge(s_wq, 32 * (layer(u) + 1))
                    wait(pe, s_eqhi, u)
                    product(q_ps, KH, lambda a, k, o: wview(Wc, a, 0, k, o * P, P), lambda b, k: hT[:, b, k, :], s_q)
                if have(t):
                    pe.wait_ge(s_eqT, t + 1)
                    pe.wait_ge(s_klo, t + 1)
                    wait(pe, s_mlo, t)
                    product(m_ps, KH, lambda a, k, o: eqT[:, a, k, blk(o)], lambda b, k: khl[:, b, k, :], s_m)
                if have(u):
                    pe.wait_ge(s_wk, 32 * (layer(u) + 1))
                    wait(pe, s_ek, u)
                    product(k_ps, TB, lambda a, k, o: hT[:, a, k, blk(o)], lambda b, k: wview(Wc, b, 1, k, 0, D), s_k)
                if have(t):
                    pe.wait_ge(s_mlo, t + 1)
                    pe.wait_ge(s_wo, 32 * (layer(t) + 1))
                    wait(pe, s_plo, t)
                    product(p_ps, KH, lambda a, k, o: MT[:, a, k, blk(o)], lambda b, k: wview(Wc, b, 3, k, 0, D), s_p)
                if have(u):
                    pe.wait_ge(s_wv, 32 * (layer(u) + 1))
                    wait(pe, s_vlo, u)
                    product(v_ps, KH, lambda a, k, o: wview(Wc, a, 2, k, o * P, P), lambda b, k: hT[:, b, k, :], s_v)
                if have(t + 2):
                    pe.wait_ge(s_h, t + 3)
                    wait(pe, s_hT, t + 2)
                    flip(hT_ps, hhl, s_th)
                if have(u):
                    pe.wait_ge(s_eqlo, u + 1)
                    wait(pe, s_eqT, u)
                    flip(eqT_ps, EQhl, s_tq)
                if have(t):
                    pe.wait_ge(s_plo, t + 1)
                    pe.wait_ge(s_vlo, t + 1)
                    wait(pe, s_x, t + NB)
                    product(o_ps, TB, lambda a, k, o: vT[:, a, k, blk(o)], lambda b, k: PR[:, b, k, :], s_o)

            item_loop(pe, one, 2)

            pe.wait_ge(s_x, NB + ITEMS)
            pe.wait_ge(s_gw, 16)
            for g in range(NG4):
                pe.wait_ge(s_xf, g + 1)
                if g:
                    pe.wait_ge(s_xT32, 2 * g)
                for k in range(KH):
                    for t in range(4):
                        last = nc.tensor.transpose(pb[k][:, t * P:(t + 1) * P], xf[:, g % 2, t, k * P:(k + 1) * P], ident[:, :])
                last.then_inc(s_xfT, 1)
                pe.wait_ge(s_xT32, 2 * (g + 1))
                if g:
                    pe.wait_ge(s_gcp, g)
                for t in range(4):
                    for k in range(KH):
                        last = mm(pb[2][:, t * E:(t + 1) * E], xT32[:, g % 2, k, t * P:(t + 1) * P], gw[:, k, :],
                                  start=(k == 0), stop=(k == 1))
                last.then_inc(s_gate, 1)
            pe.wait_ge(s_gcp, NG4)
            pe.wait_ge(s_xTlo, NG4)

            def up(i, p):
                e, tile = i // NT, i % NT
                if not (isinstance(i, int) and i < 2):
                    pe.wait_ge(s_g, i - 1)
                for w in range(2):
                    for c in range(HC):
                        n_ = 0
                        for a, b in PARTS:
                            W = (W12h, W12l)[a]
                            for k in range(KH):
                                last = mm(pb[2 * p + w][:, c * P:(c + 1) * P],
                                          W[:, bass.ds(e, 1), k, w * HID + c * P:w * HID + (c + 1) * P].rearrange("p a n -> p (a n)"),
                                          xT[:, b, k, bass.ds(tile * P, P)], start=(n_ == 0), stop=(n_ == 5))
                                n_ += 1
                last.then_inc(s_h12, 1)

            def down(i, p):
                e = i // NT
                pe.wait_ge(s_glo, i + 1)
                if not (isinstance(i, int) and i < 2):
                    pe.wait_ge(s_acc, i - 1)
                n_ = 0
                for a, b in PARTS:
                    W = (W3h, W3l)[b]
                    for c in range(HC):
                        last = mm(pb[4 + p][:, 0:D], gThl[:, p, a, c, :], W[:, bass.ds(e, 1), c, :].rearrange("p a n -> p (a n)"),
                                  start=(n_ == 0), stop=(n_ == 11))
                        n_ += 1
                last.then_inc(s_y, 1)

            NI = NE * NT
            up(0, 0)
            up(1, 1)
            down(0, 0)
            with pe.Fori(1, NI // 2) as h:
                i = pe.snap(h * 2)
                up(i, 0)
                down(pe.snap(i - 1), 1)
                up(pe.snap(i + 1), 1)
                down(i, 0)
            down(NI - 1, 1)

        @block.scalar
        def _(act):
            A = nc.scalar.activation
            for e in range(NE):
                act.wait_ge(s_fstage[e % 2], 48 * (e // 2 + 1))
                A(W12h[:, e, :, :].rearrange("p k n -> p (k n)"), FST[e % 2][:, 0:FW12], ACT.Copy, scale=WS)
                A(W3h[:, e, :, :].rearrange("p k n -> p (k n)"), FST[e % 2][:, FW12:], ACT.Copy, scale=WS).then_inc(s_fhi, 1)
            n = steps(act)

            def chunk(step, v0, j):
                act.wait_ge(s_wtr[j], step + 1)
                if not (isinstance(step, int) and step == 0):
                    act.wait_ge(s_wst[j], step * 16)
                A(VR[j][:, 0:2, :].rearrange("p a b -> p (a b)"), pb[2 * j][:, :], ACT.Copy).then_inc(s_wcp[j], 1)
                act.wait_ge(s_wcp[j], (step + 1) * 2)
                act.wait_ge(s_reuse, step // STRETCH + 1)
                act.dma_start(emb_rows[bass.ds(v0, VCH), :].rearrange("(v p) d -> p v d", p=P), VR[j][:, :, :]).then_inc(s_wst[j], 16)

            for j in range(VBUF):
                chunk(0, j * VCH, j)
            with act.Fori(1, n) as step:
                for j in range(VBUF):
                    r0 = first_column(act, step, j) - (step // STRETCH) * VROWS
                    chunk(step, act.snap(r0).with_bounds(min_val=0, max_val=VROWS - VCH, guaranteed_mod_val=0, out_of_modulus=1), j)


            def cut(n, l, s):
                at = bass.ds(s * WSN, WSN)
                act.wait_ge(s_wstage, 32 * (l + 1))
                wait(act, s_wnlo, n)
                A(Wsc[:, :], Wst[:, at], ACT.Copy, scale=WS).then_inc(s_wsc, 1)
                act.wait_ge(s_wsc, n + 1)
                if not (isinstance(l, int) and l == 0):
                    act.wait_ge(s_wo, 32 * l)
                A(Wn[:, 0, at], Wsc[:, :], ACT.Copy).then_inc(s_wnhi, 1)

            for n_ in range(WSL):
                cut(n_, 0, n_)

            def one(t, prep):
                u = t + 1
                if have(t):
                    act.wait_ge(s_v, t + 1)
                    wait(act, s_o, t)
                    A(vT[:, 0, :, :], v_ps, ACT.Copy, scale=1.0 / WS).then_inc(s_vhi, 1)
                if have(u):
                    act.wait_ge(s_nqmax, u + 1)
                    wait(act, s_eqlo, u)
                    wait(act, s_rzq, u)
                    for k in range(KH):
                        last = A(EQ[:, k, :], q_ps[:, k, :], ACT.Exp, bias=nqmax[:, k:k + 1], scale=1.0 / WS, accum_out=zq[:, k:k + 1])
                    last.then_inc(s_eq, 1)
                if have(t):
                    act.wait_ge(s_m, t + 1)
                    act.wait_ge(s_rzq, t + 1)
                    wait(act, s_p, t)
                    for k in range(KH):
                        last = A(MT[:, 0, k, :], m_ps[:, k, :], ACT.Copy, scale=rzq[:, k:k + 1])
                    last.then_inc(s_mhi, 1)
                if have(u):
                    wait(act, s_tq, u)
                    for k in range(KH):
                        last = A(EQhl[:, 0, k, :], q_ps[:, k, :], ACT.Exp, bias=nqmax[:, k:k + 1], scale=1.0 / WS)
                    last.then_inc(s_eqhi, 1)
                    act.wait_ge(s_nkmax, u + 1)
                    wait(act, s_klo, u)
                    for k in range(TB):
                        last = A(EK[:, k, :], k_ps[:, k, :], ACT.Exp, bias=nkmax[:, k:k + 1], scale=1.0 / WS, accum_out=zk[:, k:k + 1])
                    last.then_inc(s_ek, 1)
                if have(t):
                    act.wait_ge(s_p, t + 1)
                    wait(act, s_o, t)
                    A(PR[:, 0, :, :], p_ps, ACT.Copy, scale=PS / (KS * WS)).then_inc(s_phi, 1)
                if have(t + 2):
                    act.wait_ge(s_th, t + 3)
                    A(hT[:, :, :, :], hT_ps, ACT.Copy).then_inc(s_hT, 1)
                if have(u):
                    act.wait_ge(s_tq, u + 1)
                    A(eqT[:, :, :, :], eqT_ps, ACT.Copy).then_inc(s_eqT, 1)
                if prep:
                    l = layer(t) + 1
                    cut(t + WSL if isinstance(t, int) else act.snap(WSL * l + t % WSL), l, t % WSL)

            item_loop(act, one, 2, prepare=True)

            for g in range(NG4):
                act.wait_ge(s_xfT, g + 1)
                if g >= 2:
                    act.wait_ge(s_xTlo, g - 1)
                    act.wait_ge(s_gate, g - 1)
                for k in range(KH):
                    A(xT32[:, g % 2, k, :], pb[k][:, :], ACT.Copy).then_inc(s_xT32, 1)
                act.wait_ge(s_xT32, 2 * (g + 1))
                for k in range(KH):
                    last = A(xT[:, 0, k, g * 4 * P:(g + 1) * 4 * P], xT32[:, g % 2, k, :], ACT.Copy)
                last.then_inc(s_xThi, 1)
            act.wait_ge(s_gap, 1)
            A(gexp[:, :], gap[:, :], ACT.Exp).then_inc(s_gexp, 1)

            def gate(i, p):
                act.wait_ge(s_h12, i + 1)
                if not (isinstance(i, int) and i < 2):
                    act.wait_ge(s_g, i - 1)
                A(silu[:, p, :, :], pb[2 * p][:, :].rearrange("p (c n) -> p c n", c=HC), ACT.Silu, scale=1.0 / WS).then_inc(s_silu, 1)
                act.wait_ge(s_g, i + 1)
                if not (isinstance(i, int) and i < 2):
                    act.wait_ge(s_y, i - 1)
                A(gThl[:, p, 0, :, :], gT32[:, p, :, :], ACT.Copy).then_inc(s_ghi, 1)

            gate(0, 0)
            gate(1, 1)
            with act.Fori(1, NE * NT // 2) as h:
                i = act.snap(h * 2)
                gate(i, 0)
                gate(act.snap(i + 1), 1)

        @block.vector
        def _(dve):
            V = nc.vector
            dve.wait_ge(s_idrow, 16)
            V.tensor_reduce(idmax[:, 0:1], idrow[:, :], AX.X, ALU.max).then_inc(s_idmax, 1)
            dve.wait_ge(s_idmax, 1)
            for e in range(NE):
                dve.wait_ge(s_fstage[e % 2], 48 * (e // 2 + 1))
                dve.wait_ge(s_fhi, e + 1)
                V.scalar_tensor_tensor(W12l[:, e, :, :].rearrange("p k n -> p (k n)"), FST[e % 2][:, 0:FW12], WS,
                                       W12h[:, e, :, :].rearrange("p k n -> p (k n)"), ALU.mult, ALU.subtract)
                V.scalar_tensor_tensor(W3l[:, e, :, :].rearrange("p k n -> p (k n)"), FST[e % 2][:, FW12:], WS,
                                       W3h[:, e, :, :].rearrange("p k n -> p (k n)"), ALU.mult, ALU.subtract).then_inc(s_flo, 1)
            n = steps(dve)

            def chunk(step, j):
                dve.wait_ge(s_wtr[j], step + 1)
                if not (isinstance(step, int) and step == 0):
                    dve.wait_ge(s_wst[j], step * 16)
                V.tensor_copy(VR[j][:, 2:4, :].rearrange("p a b -> p (a b)"), pb[2 * j + 1][:, :]).then_inc(s_wcp[j], 1)

            for j in range(VBUF):
                chunk(0, j)
            with dve.Fori(1, n) as step:
                for j in range(VBUF):
                    chunk(step, j)

            for g in range(4):
                dve.wait_ge(s_gath[g], (n // STRETCH) * 128)
                for t in range(8 * g, 8 * g + 8):
                    V.bn_stats(stats[:, t % 8, :], X[:, t, :]).then_inc(s_st, 1)
                dve.wait_ge(s_st, 8 * (g + 1))
                for t in range(8 * g, 8 * g + 8):
                    V.bn_aggr(mv[:, t, :], stats[:, t % 8:t % 8 + 1, :]).then_inc(s_stat, 1)
                dve.wait_ge(s_h0st[g], 16)
                dve.wait_ge(s_rstd, g + 1)
                for t in range(8 * g, 8 * g + 8):
                    last = V.tensor_scalar(X[:, t, :], X[:, t, :], mv[:, t, 0:1], rstd[:, t:t + 1], ALU.subtract, ALU.mult)
                    if t % TB == TB - 1:
                        last.then_inc(s_x, 1)

            def norm(u):
                dve.wait_ge(s_arstd, u + 1)
                wait(dve, s_hhi, u)
                for k in range(TB):
                    last = V.tensor_scalar(xn[:, k, :], X[:, bass.ds(seq(u) * TB + k, 1), :].rearrange("p a n -> p (a n)"),
                                           amv[:, k, 0:1], arstd[:, k:k + 1], ALU.subtract, ALU.mult)
                last.then_inc(s_xn, 1)

            def add(t):
                dve.wait_ge(s_o, t + 1)
                dve.wait_ge(s_xb, t + 1)
                V.scalar_tensor_tensor(tiles(t), o_ps, 1.0 / PS, tiles(t), ALU.mult, ALU.add).then_inc(s_x, 1)

            def one(t, prep):
                u, w = t + 1, t + 3
                if have(t - 1):
                    add(t - 1)
                if have(t):
                    dve.wait_ge(s_vhi, t + 1)
                    V.scalar_tensor_tensor(vT[:, 1, :, :], v_ps, 1.0 / WS, vT[:, 0, :, :], ALU.mult, ALU.subtract).then_inc(s_vlo, 1)
                if have(u):
                    dve.wait_ge(s_q, u + 1)
                    V.tensor_reduce(qmax[:, :], q_ps, AX.X, ALU.max).then_inc(s_qmax, 1)
                    dve.wait_ge(s_qmax, u + 1)
                    wait(dve, s_eqhi, u)
                    V.tensor_scalar(nqmax[:, :], qmax[:, :], -1.0 / WS, None, ALU.mult).then_inc(s_nqmax, 1)
                if have(w):
                    dve.wait_ge(s_x, w + 1)
                    for k in range(TB):
                        V.bn_stats(stats[:, k, :], X[:, bass.ds(seq(w) * TB + k, 1), :].rearrange("p a n -> p (a n)")).then_inc(s_astat, 1)
                if have(t):
                    dve.wait_ge(s_mhi, t + 1)
                    if have(w):
                        dve.wait_ge(s_astat, (w + 1) * TB)
                        wait(dve, s_avar, w)
                    for k in range(KH):
                        last = V.scalar_tensor_tensor(MT[:, 1, k, :], m_ps[:, k, :], rzq[:, k:k + 1], MT[:, 0, k, :], ALU.mult, ALU.subtract)
                    last.then_inc(s_mlo, 1)
                if have(w):
                    if not have(t):
                        dve.wait_ge(s_astat, (w + 1) * TB)
                        wait(dve, s_avar, w)
                    for k in range(TB):
                        last = V.bn_aggr(amv[:, k, :], stats[:, k:k + 1, :])
                    last.then_inc(s_amv, 1)
                if have(u):
                    dve.wait_ge(s_k, u + 1)
                    V.tensor_reduce(kmax[:, :], k_ps, AX.X, ALU.max).then_inc(s_kmax, 1)
                    dve.wait_ge(s_kmax, u + 1)
                    V.tensor_scalar(nkmax[:, :], kmax[:, :], -1.0 / WS, None, ALU.mult).then_inc(s_nkmax, 1)
                    dve.wait_ge(s_eqhi, u + 1)
                    V.reciprocal(rzq[:, :], zq[:, :]).then_inc(s_rzq, 1)
                    V.tensor_tensor(EQhl[:, 1, :, :], EQ[:, :, :], EQhl[:, 0, :, :], ALU.subtract).then_inc(s_eqlo, 1)
                    dve.wait_ge(s_ek, u + 1)
                    V.reciprocal(rzk[:, :], zk[:, :]).then_inc(s_rzk, 1)
                    dve.wait_ge(s_rzk, u + 1)
                    V.tensor_scalar(rzks[:, :], rzk[:, :], KS, None, ALU.mult).then_inc(s_rzks, 1)
                    dve.wait_ge(s_rzks, u + 1)
                    wait(dve, s_m, u)
                    for k in range(TB):
                        last = V.tensor_scalar(khl[:, 0, k, :], EK[:, k, :], rzks[:, k:k + 1], None, ALU.mult)
                    last.then_inc(s_khi, 1)
                    dve.wait_ge(s_khi, u + 1)
                    for k in range(TB):
                        last = V.scalar_tensor_tensor(khl[:, 1, k, :], EK[:, k, :], rzks[:, k:k + 1], khl[:, 0, k, :], ALU.mult, ALU.subtract)
                    last.then_inc(s_klo, 1)
                if have(t):
                    dve.wait_ge(s_phi, t + 1)
                    V.scalar_tensor_tensor(PR[:, 1, :, :], p_ps, PS / (KS * WS), PR[:, 0, :, :], ALU.mult, ALU.subtract).then_inc(s_plo, 1)
                if have(w):
                    norm(w)

            item_loop(dve, one, 3)
            add(ITEMS - 1)

            dve.wait_ge(s_x, NB + ITEMS)

            def gates_out(g):
                dve.wait_ge(s_gate, g + 1)
                V.tensor_copy(gates[:, 4 * g:4 * g + 4, :], pb[2][:, 0:4 * E].rearrange("p (t e) -> p t e", t=4)).then_inc(s_gcp, 1)

            def low(g):
                dve.wait_ge(s_xThi, g + 1)
                V.tensor_tensor(xT[:, 1, :, g * 4 * P:(g + 1) * 4 * P], xT32[:, g % 2, :, :],
                                xT[:, 0, :, g * 4 * P:(g + 1) * 4 * P], ALU.subtract).then_inc(s_xTlo, 1)

            for g in range(NG4):
                xg = X[:, 4 * g:4 * g + 4, :]
                dve.wait_ge(s_h0ld[g % 2], 16 * (g // 2 + 1))
                V.tensor_tensor(xg, xg, h0b[:, g % 2, :, :], ALU.add).then_inc(s_h1, 1)
                dve.wait_ge(s_h1, g + 1)
                for t in range(4):
                    V.bn_stats(stats[:, t, :], X[:, 4 * g + t, :]).then_inc(s_st, 1)
                dve.wait_ge(s_st, NT + 4 * (g + 1))
                for t in range(4):
                    V.bn_aggr(mv[:, 4 * g + t, :], stats[:, t:t + 1, :]).then_inc(s_stat, 1)
                dve.wait_ge(s_rstd, 4 + g + 1)
                if g >= 2:
                    dve.wait_ge(s_xfT, g - 1)
                for t in range(4):
                    last = V.tensor_scalar(xf[:, g % 2, t, :], X[:, 4 * g + t, :], mv[:, 4 * g + t, 0:1], rstd[:, 4 * g + t:4 * g + t + 1],
                                           ALU.subtract, ALU.mult)
                last.then_inc(s_xf, 1)
                if g:
                    low(g - 1)
                    gates_out(g - 1)
            low(NG4 - 1)
            gates_out(NG4 - 1)

            count = [0]

            def link(ins):
                count[0] += 1
                ins.then_inc(s_route, 1)
                dve.wait_ge(s_route, count[0])

            dve.wait_ge(s_gcp, NG4)
            for t in range(NT):
                last = V.max(top8[:, t, :], gates[:, t, :])
            link(last)
            for t in range(NT):
                last = V.max_index(idx8[:, t, :], top8[:, t, :], gates[:, t, :])
            link(last)
            link(V.tensor_copy(idxf[:, :, :], idx8[:, :, :]))
            dve.wait_ge(s_iota, 1)
            link(V.tensor_copy(iota8f[:, :], iota8[:, :]))
            V.tensor_tensor(gap[:, :], top8[:, :, 1], top8[:, :, 0], ALU.subtract).then_inc(s_gap, 1)
            dve.wait_ge(s_gexp, 1)
            link(V.tensor_scalar(gden[:, :], gexp[:, :], 1.0, None, ALU.add))
            link(V.reciprocal(prob[:, 0, :], gden[:, :]))
            link(V.tensor_tensor(prob[:, 1, :], prob[:, 0, :], gexp[:, :], ALU.mult))
            for c in range(2):
                shape = [P, NT, E]
                link(V.tensor_tensor(hot[:, c, :, :], idxf[:, :, c:c + 1].broadcast_to(shape),
                                     iota8f[:, :].unsqueeze(1).broadcast_to(shape), ALU.is_equal))
                link(V.tensor_tensor(hot[:, c, :, :], hot[:, c, :, :], prob[:, c, :].unsqueeze(2).broadcast_to(shape), ALU.mult))
            link(V.tensor_tensor(hot[:, 0, :, :], hot[:, 0, :, :], hot[:, 1, :, :], ALU.add))
            link(V.memset(wexp[:, :, :], 1.0 / WS))
            link(V.tensor_scalar(wexp[:, :, 0:E], hot[:, 0, :, :], 1.0 / WS, None, ALU.mult))

            def gated(i, p):
                dve.wait_ge(s_silu, i + 1)
                if not (isinstance(i, int) and i < 2):
                    dve.wait_ge(s_ghi, i - 1)
                V.scalar_tensor_tensor(gT32[:, p, :, :], pb[2 * p + 1][:, :].rearrange("p (c n) -> p c n", c=HC), 1.0 / WS,
                                       silu[:, p, :, :], ALU.mult, ALU.mult).then_inc(s_g, 1)

            def glow(i, p):
                dve.wait_ge(s_ghi, i + 1)
                V.tensor_tensor(gThl[:, p, 1, :, :], gT32[:, p, :, :], gThl[:, p, 0, :, :], ALU.subtract).then_inc(s_glo, 1)

            def share(i, p):
                e, tile = i // NT, i % NT
                dve.wait_ge(s_y, i + 1)
                x = X[:, bass.ds(tile, 1), :].rearrange("p a n -> p (a n)")
                wcol = wexp[:, bass.ds(tile, 1), bass.ds(e, 1)].rearrange("p a n -> p (a n)")
                V.scalar_tensor_tensor(x, pb[4 + p][:, 0:D], wcol, x, ALU.mult, ALU.add).then_inc(s_acc, 1)

            gated(0, 0)
            glow(0, 0)
            gated(1, 1)
            glow(1, 1)
            share(0, 0)
            with dve.Fori(1, NE * NT // 2) as h:
                i = dve.snap(h * 2)
                gated(i, 0)
                glow(i, 0)
                share(dve.snap(i - 1), 1)
                j = dve.snap(i + 1)
                gated(j, 1)
                glow(j, 1)
                share(i, 0)
            share(NE * NT - 1, 1)


_INS = ["x", "L0_tok_W", "L0_attn_w_qkv", "L0_attn_w_out", "L0_attn_b_out", "L0_attn_gamma", "L0_attn_beta",
        "L0_ffn_gate_w", "L0_ffn_ew1", "L0_ffn_ew2", "L0_ffn_ew3", "L0_ffn_sw1", "L0_ffn_sw2", "L0_ffn_sw3"]


def kernel(**inputs):
    import concourse.bacc as _bacc
    from concourse.bass_utils import run_bass_kernel_spmd as _run

    nc = _bacc.Bacc("TRN2", target_bir_lowering=False, num_devices=1)
    arrays, args = {}, []
    for name in _INS:
        a = np.ascontiguousarray(inputs[name])
        arrays[f"in_{name}"] = a
        args.append(nc.dram_tensor(f"in_{name}", a.shape, mybir.dt.from_np(a.dtype), kind="ExternalInput").ap())
    shape = (*inputs["x"].shape, inputs["L0_tok_W"].shape[0])
    args.append(nc.dram_tensor("out_rows", shape, mybir.dt.float32, kind="ExternalOutput").ap())
    tower(nc, *args)
    return _run(nc, [arrays], core_ids=[0]).results[0]["out_rows"]
```

```python
from contextlib import ExitStack

import numpy as np

import concourse.bass as bass
from concourse import mybir

P = 128


def tower(nc, x_ids, tok_w, w_qkv, w_out, b_out, gamma, beta, gate_w, ew1, ew2, ew3, sw1, sw2, sw3, out):
    f32, f16, i32 = mybir.dt.float32, mybir.dt.float16, mybir.dt.int32
    ALU = mybir.AluOpType
    ACT = mybir.ActivationFunctionType
    AX = mybir.AxisListType

    NB, SEQ = x_ids.shape
    D, VOCAB = tok_w.shape
    DEPTH = w_qkv.shape[0]
    E, _, HID = ew1.shape
    TOK = NB * SEQ
    NT = TOK // P
    TB = SEQ // P
    KH = D // P
    HC = HID // P
    NE = E + 1
    ITEMS = DEPTH * NB
    EPS = 1e-5
    TOPK = 2
    SLOT_TILES = (TOK * TOPK + E * (P - 1)) // P + 1
    RING = 4
    assert SLOT_TILES % 2 == 0 and E * P > E * (P - 1)
    WS = 64.0
    KS = 4096.0
    PS = 256.0

    VCH = 512
    VBUF = 4
    VSTEP = VCH * VBUF
    VBLK = VCH // P
    STRETCH = 7
    VROWS = STRETCH * VSTEP
    NSTRETCH = -(-VOCAB // VROWS)

    def first_column(eng, step, j):
        v, last = step * VSTEP + j * VCH, VOCAB - VCH
        return eng.snap(v - (v > last) * (v - last)).with_bounds(min_val=0, max_val=last, guaranteed_mod_val=0, out_of_modulus=1)

    emb_rows = nc.dram_tensor("emb_rows", (VROWS, D), f32, kind="Internal").ap()
    x_rows = nc.dram_tensor("x_rows", (TOK + P, 2 * D), f16, kind="Internal").ap()
    acc_rows = nc.dram_tensor("acc_rows", (TOK + P, D), f32, kind="Internal").ap()
    slot_rows = nc.dram_tensor("slot_rows", (P * SLOT_TILES, 2), i32, kind="Internal").ap()
    h0_rows = nc.dram_tensor("h0_rows", (TOK, D), f32, kind="Internal").ap()

    def wait(eng, sem, value):
        if not (isinstance(value, int) and value <= 0):
            eng.wait_ge(sem, value)

    ctx = ExitStack()
    with ctx:
        def sb(name, shape, dt, where=ctx):
            return where.enter_context(nc.sbuf_tensor(name, shape, dt))

        def sem(name):
            return ctx.enter_context(nc.semaphore(name))

        X = sb("X", [P, NT, D], f32)
        W12h = sb("W12h", [P, NE, KH, 2 * HID], f16)
        W12l = sb("W12l", [P, NE, KH, 2 * HID], f16)
        W3h = sb("W3h", [P, NE, HC, D], f16)
        W3l = sb("W3l", [P, NE, HC, D], f16)
        ident = sb("ident", [P, P], f32)
        ident16 = sb("ident16", [P, P], f16)
        before = sb("before", [P, P], f16)
        ones16 = sb("ones16", [P, P], f16)
        idx = sb("idx", [P, NT], i32)
        epst = sb("epst", [P, TB], f32)
        mhalf = sb("mhalf", [P, NT], f32)
        stats = sb("stats", [P, 8, 6], f32)
        mv = sb("mv", [P, NT, 2], f32)
        rstd = sb("rstd", [P, NT], f32)
        h0b = sb("h0b", [P, 2, 4, D], f32)

        pb = [ctx.enter_context(nc.psum_tensor(f"bank{i}", [P, 512], f32)) for i in range(8)]

        s_ids = sem("s_ids")
        s_idrow = sem("s_idrow")
        s_const = sem("s_const")
        s_wload = [sem(f"s_wload{i}") for i in range(VBUF)]
        s_wtr = [sem(f"s_wtr{i}") for i in range(VBUF)]
        s_wcp = [sem(f"s_wcp{i}") for i in range(VBUF)]
        s_wst = [sem(f"s_wst{i}") for i in range(VBUF)]
        s_fstage = [sem(f"s_fstage{i}") for i in range(2)]
        s_fhi, s_flo = sem("s_fhi"), sem("s_flo")
        s_gath = [sem(f"s_gath{i}") for i in range(4)]
        s_h0st = [sem(f"s_h0st{i}") for i in range(4)]
        s_reuse, s_passed = sem("s_reuse"), sem("s_passed")
        s_id, s_idmax, s_wstage, s_gap = sem("s_id"), sem("s_idmax"), sem("s_wstage"), sem("s_gap")
        s_st, s_stat, s_var, s_rstd, s_norm = sem("s_st"), sem("s_stat"), sem("s_var"), sem("s_rstd"), sem("s_norm")

        NG4 = NT // 4
        emb = ExitStack()
        VW = [sb(f"VW{i}", [P, KH, VCH], f32, emb) for i in range(VBUF)]
        VR = [sb(f"VR{i}", [P, VBLK, D], f32, emb) for i in range(VBUF)]
        FST = [sb(f"FST{i}", [P, KH * 2 * HID + HC * D], f32, emb) for i in range(2)]
        idrow = W3l[0:1, :, :, :].rearrange("p e c n -> p (e c n)").bitcast(i32)[:, 0:TOK]
        idmax = sb("idmax", [1, 1], i32, emb)
        emb.close()

        FW12 = KH * 2 * HID

        att = ExitStack()
        WQKV = KH * 3 * D
        WL = WQKV + KH * D
        Wst = sb("Wst", [P, WL], f32, att)
        WSL = NB // 2
        WSN = WL // WSL
        Wsc = sb("Wsc", [P, WSN], f32, att)
        Wn = sb("Wn", [P, 2, WL], f16, att)
        Wc = sb("Wc", [P, 2, WL], f16, att)
        rows = sb("rows", [P, 2, 3, D], f32, att)
        xn = sb("xn", [P, TB, D], f32, att)
        amv = sb("amv", [P, TB, 2], f32, att)
        avar, arstd = sb("avar", [P, TB], f32, att), sb("arstd", [P, TB], f32, att)
        hf = sb("hf", [P, TB, D], f32, att)
        hhl = sb("hhl", [P, 2, TB, D], f16, att)
        hT = sb("hT", [P, 2, KH, SEQ], f16, att)
        EQ = sb("EQ", [P, KH, SEQ], f32, att)
        EQhl = sb("EQhl", [P, 2, KH, SEQ], f16, att)
        eqT = sb("eqT", [P, 2, TB, D], f16, att)
        EK = sb("EK", [P, TB, D], f32, att)
        khl = sb("khl", [P, 2, TB, D], f16, att)
        vT = sb("vT", [P, 2, KH, SEQ], f16, att)
        MT = sb("MT", [P, 2, KH, D], f16, att)
        PR = sb("PR", [P, 2, KH, D], f16, att)
        qmax, nqmax, zq, rzq = (sb(n, [P, KH], f32, att) for n in ("qmax", "nqmax", "zq", "rzq"))
        kmax, nkmax, zk, rzk, rzks = (sb(n, [P, TB], f32, att) for n in ("kmax", "nkmax", "zk", "rzk", "rzks"))
        att.close()

        s_rows = sem("s_rows")
        s_wsc, s_wnhi, s_wnlo = sem("s_wsc"), sem("s_wnhi"), sem("s_wnlo")
        s_wq, s_wk, s_wv, s_wo = sem("s_wq"), sem("s_wk"), sem("s_wv"), sem("s_wo")
        s_astat, s_amv, s_avar, s_arstd, s_xn = (sem(n) for n in ("s_astat", "s_amv", "s_avar", "s_arstd", "s_xn"))
        s_hg, s_hb, s_hhi, s_h, s_xb = (sem(n) for n in ("s_hg", "s_hb", "s_hhi", "s_h", "s_xb"))
        s_th, s_hT = sem("s_th"), sem("s_hT")
        s_q, s_qmax, s_nqmax, s_eq, s_eqhi, s_eqlo, s_tq, s_eqT, s_rzq = (
            sem(n) for n in ("s_q", "s_qmax", "s_nqmax", "s_eq", "s_eqhi", "s_eqlo", "s_tq", "s_eqT", "s_rzq"))
        s_k, s_kmax, s_nkmax, s_ek, s_rzk, s_rzks, s_khi, s_klo = (
            sem(n) for n in ("s_k", "s_kmax", "s_nkmax", "s_ek", "s_rzk", "s_rzks", "s_khi", "s_klo"))
        s_v, s_vhi, s_vlo = sem("s_v"), sem("s_vhi"), sem("s_vlo")
        s_m, s_mhi, s_mlo = sem("s_m"), sem("s_mhi"), sem("s_mlo")
        s_p, s_phi, s_plo = sem("s_p"), sem("s_phi"), sem("s_plo")
        s_o, s_x = sem("s_o"), sem("s_x")

        b_h, b_q, b_k, b_v, b_e, b_m, b_p, b_o = pb
        hT_ps = b_h[:, :].bitcast(f16).rearrange("p (a k n) -> p a k n", a=2, k=KH)
        eqT_ps = b_e[:, :].bitcast(f16).rearrange("p (a k n) -> p a k n", a=2, k=TB)
        q_ps = b_q[:, :].rearrange("p (k n) -> p k n", k=KH)
        k_ps = b_k[:, :].rearrange("p (k n) -> p k n", k=TB)
        v_ps = b_v[:, :].rearrange("p (k n) -> p k n", k=KH)
        m_ps = b_m[:, :].rearrange("p (k n) -> p k n", k=KH)
        p_ps = b_p[:, :].rearrange("p (k n) -> p k n", k=KH)
        o_ps = b_o[:, :].rearrange("p (k n) -> p k n", k=TB)

        ffn = ExitStack()
        xT = sb("xT", [P, 2, KH, TOK], f16, ffn)
        gw = sb("gw", [P, KH, E], f32, ffn)
        gwp = sb("gwp", [P, 2, KH, E], f16, ffn)
        zrow = sb("zrow", [P, D], f32, ffn)
        gates = sb("gates", [P, NT, E], f32, ffn)
        iota8 = sb("iota8", [P, E], i32, ffn)
        pay = sb("pay", [P, TOPK, NT, 2], i32, ffn)
        blank = sb("blank", [P, SLOT_TILES, 2], i32, ffn)
        iota_t = sb("iota_t", [1, SLOT_TILES], i32, ffn)
        pre = ExitStack()
        xf = sb("xf", [P, 2, 4, D], f32, pre)
        xhl = sb("xhl", [P, 2, 4, 2, D], f16, pre)
        pre.close()
        top8 = sb("top8", [P, NT, 8], f32, ffn)
        idx8 = sb("idx8", [P, NT, 8], mybir.dt.uint32, ffn)
        idxf = sb("idxf", [P, NT, 8], f32, ffn)
        iota8f = sb("iota8f", [P, E], f32, ffn)
        gap, gexp, gden = (sb(n, [P, NT], f32, ffn) for n in ("gap", "gexp", "gden"))
        prob = sb("prob", [P, 2, NT], f32, ffn)
        mask = sb("mask", [P, NT, E], f16, ffn)
        totals = sb("totals", [P, NT, E], f32, ffn)
        place = sb("place", [P, NT, E], f32, ffn)
        counti = sb("counti", [P, 3, E], i32, ffn)
        ends = sb("ends", [P, 5, E], f32, ffn)
        slotf = sb("slotf", [P, TOPK, NT], f32, ffn)
        sloti = sb("sloti", [P, 3, TOPK, NT], i32, ffn)
        slots = sb("slots", [P, SLOT_TILES, 2], i32, ffn)
        iota_tf = sb("iota_tf", [1, SLOT_TILES], f32, ffn)
        texpf = sb("texpf", [1, 2, SLOT_TILES], f32, ffn)
        ROUNDS = SLOT_TILES // RING
        packf = sb("packf", [1, 2, ROUNDS], f32, ffn)
        texp = sb("texp", [1, ROUNDS], i32, ffn)
        silu = sb("silu", [P, 2, HC, P], f32, ffn)
        gT32 = sb("gT32", [P, 2, HC, P], f32, ffn)
        gThl = sb("gThl", [P, 2, 2, HC, P], f16, ffn)
        scan = h0b[:, 0, 0:2, :].rearrange("p c (t e) -> p c t e", t=NT)
        hot = h0b[:, 0, 2:4, :].rearrange("p c (t e) -> p c t e", t=NT)
        past = h0b[0:1, 1, :, :].rearrange("p a n -> p (a n)")[:, 0:SLOT_TILES * E].rearrange("p (t e) -> p t e", e=E)
        xg = [h0b[:, i // 2, i % 2 + (i // 2) * 2, :].bitcast(f16) for i in range(RING)]
        xTg = h0b[:, 0, 2:4, :].bitcast(f16).rearrange("p w (a k n) -> p w a k n", a=2, k=KH)
        yout = h0b[:, 1, 0:2, :]
        ffn.close()
        s_fst, s_fmv, s_fvar, s_frstd, s_xf = (sem(n) for n in ("s_fst", "s_fmv", "s_fvar", "s_frstd", "s_xf"))
        s_fxhi, s_fxlo, s_fT, s_xT, s_gw, s_gwhi, s_gwlo, s_gate, s_gcp = (
            sem(n) for n in ("s_fxhi", "s_fxlo", "s_fT", "s_xT", "s_gw", "s_gwhi", "s_gwlo", "s_gate", "s_gcp"))
        s_xst = [sem(f"s_xst{i}") for i in range(2)]
        s_pad, s_ffnc, s_blank, s_mask, s_rank, s_rankcp, s_texp, s_pay, s_scat, s_slots, s_accinit = (
            sem(n) for n in ("s_pad", "s_ffnc", "s_blank", "s_mask", "s_rank", "s_rankcp", "s_texp", "s_pay", "s_scat",
                             "s_slots", "s_accinit"))
        s_xg = [sem(f"s_xg{i}") for i in range(RING)]
        s_tx, s_txcp, s_yout, s_sadd = sem("s_tx"), sem("s_txcp"), sem("s_yout"), sem("s_sadd")
        s_route = sem("s_route")
        s_gexp, s_iota = sem("s_gexp"), sem("s_iota")
        s_h12, s_silu, s_g, s_ghi, s_glo, s_y, s_acc = (
            sem(n) for n in ("s_h12", "s_silu", "s_g", "s_ghi", "s_glo", "s_y", "s_acc"))
        s_h0ld = [sem(f"s_h0ld{i}") for i in range(4)]
        s_h1 = sem("s_h1")
        s_out = sem("s_out")


        block = ctx.enter_context(nc.Block())

        def stretches(eng):
            eng.wait_ge(s_idmax, 1)
            return eng.snap(eng.value_load(idmax[0:1, 0:1], min_val=0, max_val=VOCAB - 1) // VROWS + 1)

        def steps(eng):
            return eng.snap(stretches(eng) * STRETCH)

        def layer(u):
            return u // NB

        def seq(u):
            return u % NB

        def tiles(u):
            return X[:, bass.ds(seq(u) * TB, TB), :]

        def wview(w, part, j, k, c0, n):
            at = k * 3 * D + j * D + c0 if j < 3 else WQKV + k * D + c0
            return w[:, part, at:at + n]

        PARTS = [(0, 0), (0, 1), (1, 0)]

        def item_loop(eng, one, lead, prepare=False):
            for t in range(-lead, 1):
                one(t, prepare and t == 0)
            if not prepare:
                with eng.Fori(1, ITEMS - lead) as t:
                    one(t, False)
            else:
                with eng.Fori(1, NB // 2) as t:
                    one(t, True)
                with eng.Fori(NB // 2, NB) as t:
                    one(t, False)
                with eng.Fori(1, DEPTH - 1) as l:
                    with eng.Fori(0, NB // 2) as b:
                        one(eng.snap(l * NB + b), True)
                    with eng.Fori(NB // 2, NB) as b:
                        one(eng.snap(l * NB + b), False)
                with eng.Fori(ITEMS - NB, ITEMS - lead) as t:
                    one(t, False)
            for t in range(ITEMS - lead, ITEMS):
                one(t, False)

        EARLY = 2

        def have(u):
            return not isinstance(u, int) or 0 <= u < ITEMS

        @block.sync
        def _(sp):
            sp.dma_start(idrow[:, :], x_ids.rearrange("b s -> (b s)").rearrange("(a n) -> a n", a=1)).then_inc(s_idrow, 16)
            with nc.allow_non_contiguous_dma(reason="16 KB of token ids"):
                sp.dma_start(idx[:, :], x_ids.rearrange("b (t p) -> p (b t)", p=P)).then_inc(s_ids, 16)
            def load_expert(e):
                if e >= 2:
                    sp.wait_ge(s_flo, e - 1)
                w1, w2, w3 = (ew1[e], ew2[e], ew3[e]) if e < E else (sw1, sw2, sw3)
                st = FST[e % 2]
                st12 = st[:, 0:FW12].rearrange("p (k w n) -> p k w n", k=KH, w=2)
                sp.dma_start(st12[:, :, 0, :], w1.rearrange("(k p) n -> p k n", p=P)).then_inc(s_fstage[e % 2], 16)
                sp.dma_start(st12[:, :, 1, :], w2.rearrange("(k p) n -> p k n", p=P)).then_inc(s_fstage[e % 2], 16)
                sp.dma_start(st[:, FW12:].rearrange("p (c n) -> p c n", c=HC),
                             w3.rearrange("(c p) n -> p c n", p=P)).then_inc(s_fstage[e % 2], 16)
            for e in range(EARLY):
                load_expert(e)
            src = tok_w.rearrange("(k p) v -> p k v", p=P)

            def load(step, v0, j):
                if not isinstance(step, int):
                    sp.wait_ge(s_wtr[j], step)
                sp.dma_start(VW[j][:, :, :], src[:, :, bass.ds(v0, VCH)]).then_inc(s_wload[j], 16)

            for j in range(VBUF):
                load(0, j * VCH, j)
            for e in range(EARLY, EARLY + 2):
                load_expert(e)
            n = steps(sp)
            with sp.Fori(1, n) as step:
                for j in range(VBUF):
                    load(step, first_column(sp, step, j), j)
            for e in range(EARLY + 2, NE):
                load_expert(e)
            for g in range(4):
                sp.wait_ge(s_gath[g], (n // STRETCH) * (16 * NT // 4))
                sp.dma_start(h0_rows.rearrange("(t p) d -> p t d", p=P)[:, g * NT // 4:(g + 1) * NT // 4, :],
                             X[:, g * NT // 4:(g + 1) * NT // 4, :]).then_inc(s_h0st[g], 16)
            sp.wait_ge(s_flo, NE)
            for l in range(DEPTH):
                if l:
                    sp.wait_ge(s_wsc, WSL * l)
                sp.dma_start(Wst[:, 0:WQKV].rearrange("p (k n) -> p k n", k=KH),
                             w_qkv[l].rearrange("(k p) n -> p k n", p=P)).then_inc(s_wstage, 16)
                sp.dma_start(Wst[:, WQKV:].rearrange("p (k n) -> p k n", k=KH),
                             w_out[l].rearrange("(k p) n -> p k n", p=P)).then_inc(s_wstage, 16)
                if l:
                    sp.wait_ge(s_xb, NB * (l - 1) + 1)
                for r, v in enumerate((gamma, beta, b_out)):
                    sp.dma_start(rows[:, l % 2, r, :], v[l:l + 1, :].broadcast_to([P, D])).then_inc(s_rows, 16)
                sp.wait_ge(s_wnlo, WSL * (l + 1))
                for j, (used, ready) in enumerate(((s_q, s_wq), (s_k, s_wk), (s_v, s_wv), (s_p, s_wo))):
                    if l:
                        sp.wait_ge(used, NB * l)
                    if j < 3:
                        part = lambda w, a: w[:, a, 0:WQKV].rearrange("p (k j n) -> p k j n", k=KH, j=3)[:, :, j, :]
                    else:
                        part = lambda w, a: w[:, a, WQKV:]
                    for a in range(2):
                        sp.dma_start(part(Wc, a), part(Wn, a)).then_inc(ready, 16)
            def load_h0(g):
                if g >= 2:
                    sp.wait_ge(s_h1, g - 1)
                sp.dma_start(h0b[:, g % 2, :, :], h0_rows.rearrange("(t p) d -> p t d", p=P)[:, 4 * g:4 * g + 4, :])\
                  .then_inc(s_h0ld[g % 2], 16)

            sp.wait_ge(s_h0st[3], 16)
            load_h0(0)
            load_h0(1)
            sp.wait_ge(s_ffnc, 1)
            sp.dma_start(gw[:, :, :], gate_w.rearrange("(k p) e -> p k e", p=P)).then_inc(s_gw, 16)
            sp.dma_start(slot_rows.rearrange("(p t) c -> p (t c)", p=P), blank[:, :, :].rearrange("p t c -> p (t c)")).then_inc(s_blank, 16)
            sp.dma_start(acc_rows[TOK:TOK + P, :], zrow[:, :]).then_inc(s_pad, 16)
            sp.dma_start(x_rows[TOK:TOK + P, :], zrow[:, :].bitcast(f16)).then_inc(s_pad, 16)
            for g in range(NG4):
                if g + 2 < NG4:
                    load_h0(g + 2)
                sp.wait_ge(s_fxlo, g + 1)
                sp.dma_start(x_rows[g * 4 * P:(g + 1) * 4 * P, :].rearrange("(t p) d -> p t d", p=P),
                             xhl[:, g % 2, :, :, :].rearrange("p t a d -> p t (a d)")).then_inc(s_xst[g % 2], 16)
            sp.wait_ge(s_scat, 16 * TOPK * NT)
            sp.dma_start(slots[:, :, :].rearrange("p t c -> p (t c)"), slot_rows.rearrange("(p t) c -> p (t c)", p=P)).then_inc(s_slots, 16)
            for g in range(NG4):
                sp.wait_ge(s_acc, 4 * (g + 1))
                sp.dma_start(acc_rows[g * 4 * P:(g + 1) * 4 * P, :].rearrange("(t p) d -> p t d", p=P),
                             X[:, 4 * g:4 * g + 4, :]).then_inc(s_accinit, 16)
            sp.wait_ge(s_sadd, 16 * SLOT_TILES)
            flat = out.rearrange("b s d -> (b s) d")
            for g in range(4):
                at = slice(g * TOK // 4, (g + 1) * TOK // 4)
                sp.dma_start(flat[at, :], acc_rows[at, :]).then_inc(s_out, 16)
            sp.wait_ge(s_out, 64)

        @block.gpsimd
        def _(pool):
            pool.memset(ident[:, :], 0.0).then_inc(s_id, 1)
            pool.memset(mhalf[:, :], -0.5)
            pool.wait_ge(s_id, 1)
            pool.affine_select(out=ident[:, :], in_=ident[:, :], compare_op=ALU.not_equal, fill=1.0, base=0,
                               pattern=[[-1, P]], channel_multiplier=1).then_inc(s_id, 1)
            pool.wait_ge(s_id, 2)
            pool.tensor_copy(ident16[:, :], ident[:, :])
            pool.memset(ones16[:, :], 1.0).then_inc(s_id, 1)
            pool.wait_ge(s_id, 3)
            pool.affine_select(out=before[:, :], in_=ones16[:, :], compare_op=ALU.is_gt, fill=0.0, base=0,
                               pattern=[[1, P]], channel_multiplier=-1).then_inc(s_const, 1)
            pool.memset(epst[:, :], EPS)
            pool.wait_ge(s_ids, 16)
            pool.sem_inc(s_reuse, 1)
            with pool.Fori(0, stretches(pool)) as q:
                for j in range(VBUF):
                    pool.wait_ge(s_wst[j], (q + 1) * (STRETCH * 16))
                pool.sem_inc(s_passed, 1)
                for t in range(NT):
                    pool.indirect_dma_start(out=X[:, t, :], out_offset=None, in_=emb_rows,
                                            in_offset=bass.IndirectOffsetOnAxis(ap=idx[:, t:t + 1], axis=0),
                                            bounds_check=VROWS - 1, oob_is_err=False)\
                        .then_inc(s_gath[t // 8], 16)
                for g in range(4):
                    pool.wait_ge(s_gath[g], (q + 1) * 128)
                pool.sem_inc(s_passed, 1)
                pool.tensor_scalar(idx[:, :], idx[:, :], -VROWS, None, ALU.add).then_inc(s_reuse, 1)
                pool.wait_ge(s_reuse, q + 2)
                pool.sem_inc(s_passed, 1)

            def cut(n):
                lo = bass.ds((n % WSL) * WSN, WSN)
                pool.wait_ge(s_wnhi, n + 1)
                pool.sem_inc(s_passed, 1)
                pool.tensor_tensor(Wn[:, 1, lo], Wsc[:, :], Wn[:, 0, lo], ALU.subtract).then_inc(s_wnlo, 1)

            for g in range(4):
                pool.wait_ge(s_stat, 8 * (g + 1))
                v = mv[:, 8 * g:8 * g + 8, 1]
                pool.tensor_scalar(v, v, EPS, None, ALU.add).then_inc(s_var, 1)
                pool.wait_ge(s_var, g + 1)
                pool.tensor_tensor(rstd[:, 8 * g:8 * g + 8], v, mhalf[:, 0:8], ALU.pow).then_inc(s_rstd, 1)
                for n in range(WSL * max(g - 1, 0) // 3, WSL * g // 3):
                    cut(n)

            def one(t, prep):
                u = t + 3
                if have(u):
                    pool.wait_ge(s_amv, u + 1)
                    pool.tensor_tensor(avar[:, :], amv[:, :, 1], epst[:, :], ALU.add).then_inc(s_avar, 1)
                    pool.wait_ge(s_avar, u + 1)
                    wait(pool, s_xn, u)
                    pool.tensor_tensor(arstd[:, :], avar[:, :], mhalf[:, 0:TB], ALU.pow).then_inc(s_arstd, 1)
                    pool.wait_ge(s_rows, 48 * (layer(u) + 1))
                    pool.wait_ge(s_xn, u + 1)
                    pool.sem_inc(s_passed, 1)
                    row = lambda r: rows[:, bass.ds(layer(u) % 2, 1), r, :].broadcast_to([P, TB, D])
                    pool.tensor_tensor(xn[:, :, :], xn[:, :, :], row(0), ALU.mult).then_inc(s_hg, 1)
                    pool.wait_ge(s_hg, u + 1)
                    wait(pool, s_th, u)
                    pool.sem_inc(s_passed, 1)
                    pool.tensor_tensor(hf[:, :, :], xn[:, :, :], row(1), ALU.add)
                    pool.tensor_tensor(hhl[:, 0, :, :], xn[:, :, :], row(1), ALU.add).then_inc(s_hhi, 1)
                    pool.wait_ge(s_hhi, u + 1)
                    pool.tensor_tensor(hhl[:, 1, :, :], hf[:, :, :], hhl[:, 0, :, :], ALU.subtract).then_inc(s_h, 1)
                    pool.tensor_tensor(tiles(u), tiles(u), row(2), ALU.add).then_inc(s_xb, 1)
                if prep:
                    cut(t + WSL if isinstance(t, int) else pool.snap(WSL * (layer(t) + 1) + t % WSL))

            item_loop(pool, one, 3, prepare=True)
            pool.wait_ge(s_x, NB + ITEMS)
            pool.iota(iota8[:, :], pattern=[[1, E]], base=0, channel_multiplier=0)
            pool.iota(iota_t[:, :], pattern=[[1, SLOT_TILES]], base=0, channel_multiplier=0)
            for c in range(TOPK):
                pool.iota(pay[:, c, :, 0], pattern=[[P, NT]], base=0, channel_multiplier=1)
            pool.iota(blank[:, :, 0], pattern=[[0, SLOT_TILES]], base=TOK, channel_multiplier=1)
            pool.memset(blank[:, :, 1], 0)
            pool.memset(zrow[:, :], 0.0).then_inc(s_ffnc, 1)

            def low(g):
                pool.wait_ge(s_fxhi, g + 1)
                pool.tensor_tensor(xhl[:, g % 2, :, 1, :], xf[:, g % 2, :, :], xhl[:, g % 2, :, 0, :], ALU.subtract).then_inc(s_fxlo, 1)

            for g in range(NG4):
                pool.wait_ge(s_stat, NT + 4 * (g + 1))
                v = mv[:, 4 * g:4 * g + 4, 1]
                pool.tensor_scalar(v, v, EPS, None, ALU.add).then_inc(s_var, 1)
                pool.wait_ge(s_var, 4 + g + 1)
                pool.tensor_tensor(rstd[:, 4 * g:4 * g + 4], v, mhalf[:, 0:4], ALU.pow).then_inc(s_rstd, 1)
                if g:
                    low(g - 1)
            low(NG4 - 1)
            pool.wait_ge(s_pay, 1)
            pool.wait_ge(s_blank, 16)
            for c in range(TOPK):
                for t in range(NT):
                    pool.indirect_dma_start(out=slot_rows, out_offset=bass.IndirectOffsetOnAxis(ap=sloti[:, 2, c, t:t + 1], axis=0),
                                            in_=pay[:, c, t, :], in_offset=None).then_inc(s_scat, 16)
            pool.wait_ge(s_slots, 16)
            for w in range(2):
                pool.wait_ge(s_xst[w], 16 * NG4 // 2)
            pool.wait_ge(s_pad, 32)

            def gather(j):
                if j >= RING:
                    pool.wait_ge(s_tx, j - RING + 1)
                pool.indirect_dma_start(out=xg[j % RING], out_offset=None, in_=x_rows,
                                        in_offset=bass.IndirectOffsetOnAxis(ap=slots[:, j, 0:1], axis=0)).then_inc(s_xg[j % RING], 16)

            pool.wait_ge(s_texp, 1)
            for j in range(RING - 1):
                gather(j)
            for j in range(SLOT_TILES):
                if j + RING - 1 < SLOT_TILES:
                    gather(j + RING - 1)
                pool.wait_ge(s_yout, j + 1)
                if j == 0:
                    pool.wait_ge(s_accinit, 16 * NG4)
                else:
                    pool.wait_ge(s_sadd, 16 * j)
                pool.indirect_dma_start(out=acc_rows, out_offset=bass.IndirectOffsetOnAxis(ap=slots[:, j, 0:1], axis=0),
                                        in_=yout[:, j % 2, :], in_offset=None, compute_op=ALU.add).then_inc(s_sadd, 16)

        @block.tensor
        def _(pe):
            mm = nc.tensor.matmul
            pe.wait_ge(s_const, 1)
            n = steps(pe)

            def chunk(step, j):
                pe.wait_ge(s_wload[j], (step + 1) * 16)
                if not (isinstance(step, int) and step == 0):
                    pe.wait_ge(s_wcp[j], step * 2)
                for v in range(VBLK):
                    for k in range(KH):
                        last = nc.tensor.transpose(pb[2 * j + v // 2][:, (v % 2) * D + k * P:(v % 2) * D + k * P + P],
                                                   VW[j][:, k, v * P:(v + 1) * P], ident[:, :])
                last.then_inc(s_wtr[j], 1)

            for j in range(VBUF):
                chunk(0, j)
            with pe.Fori(1, n) as step:
                for j in range(VBUF):
                    chunk(step, j)
            for j in range(VBUF):
                pe.wait_ge(s_wcp[j], n * 2)

            def product(dst, m, lhs, rhs, sem_):
                for o in range(m):
                    last = None
                    for i, (a, b) in enumerate(PARTS):
                        for k in range(2):
                            last = mm(dst[:, o, :], lhs(a, k, o), rhs(b, k), start=(i == 0 and k == 0), stop=(i == 2 and k == 1))
                last.then_inc(sem_, 1)

            def flip(dst, src, sem_):
                for a in range(2):
                    for k in range(2):
                        for t in range(2):
                            last = nc.tensor.transpose(dst[:, a, k, t * P:(t + 1) * P], src[:, a, t, k * P:(k + 1) * P], ident16[:, :])
                last.then_inc(sem_, 1)

            blk = lambda o: slice(o * P, (o + 1) * P)

            def one(t, prep):
                u = t + 1
                if have(u):
                    pe.wait_ge(s_hT, u + 1)
                    pe.wait_ge(s_wq, 32 * (layer(u) + 1))
                    wait(pe, s_eqhi, u)
                    product(q_ps, KH, lambda a, k, o: wview(Wc, a, 0, k, o * P, P), lambda b, k: hT[:, b, k, :], s_q)
                if have(t):
                    pe.wait_ge(s_eqT, t + 1)
                    pe.wait_ge(s_klo, t + 1)
                    wait(pe, s_mlo, t)
                    product(m_ps, KH, lambda a, k, o: eqT[:, a, k, blk(o)], lambda b, k: khl[:, b, k, :], s_m)
                if have(u):
                    pe.wait_ge(s_wk, 32 * (layer(u) + 1))
                    wait(pe, s_ek, u)
                    product(k_ps, TB, lambda a, k, o: hT[:, a, k, blk(o)], lambda b, k: wview(Wc, b, 1, k, 0, D), s_k)
                if have(t + 2):
                    pe.wait_ge(s_h, t + 3)
                    wait(pe, s_hT, t + 2)
                    flip(hT_ps, hhl, s_th)
                if have(t):
                    pe.wait_ge(s_mlo, t + 1)
                    pe.wait_ge(s_wo, 32 * (layer(t) + 1))
                    wait(pe, s_plo, t)
                    product(p_ps, KH, lambda a, k, o: MT[:, a, k, blk(o)], lambda b, k: wview(Wc, b, 3, k, 0, D), s_p)
                if have(u):
                    pe.wait_ge(s_wv, 32 * (layer(u) + 1))
                    wait(pe, s_vlo, u)
                    product(v_ps, KH, lambda a, k, o: wview(Wc, a, 2, k, o * P, P), lambda b, k: hT[:, b, k, :], s_v)
                if have(u):
                    pe.wait_ge(s_eqlo, u + 1)
                    wait(pe, s_eqT, u)
                    flip(eqT_ps, EQhl, s_tq)
                if have(t):
                    pe.wait_ge(s_plo, t + 1)
                    pe.wait_ge(s_vlo, t + 1)
                    wait(pe, s_x, t + NB)
                    product(o_ps, TB, lambda a, k, o: vT[:, a, k, blk(o)], lambda b, k: PR[:, b, k, :], s_o)

            item_loop(pe, one, 2)

            pe.wait_ge(s_x, NB + ITEMS)
            pe.wait_ge(s_gwlo, 1)

            def turn(g):
                pe.wait_ge(s_fxlo, g + 1)
                if g >= 2:
                    pe.wait_ge(s_xT, 2 * (g - 1))
                for a in range(2):
                    dst = pb[2 * (g % 2) + a][:, :].bitcast(f16).rearrange("p (k n) -> p k n", k=KH)
                    for k in range(KH):
                        for t in range(4):
                            last = nc.tensor.transpose(dst[:, k, t * P:(t + 1) * P], xhl[:, g % 2, t, a, k * P:(k + 1) * P], ident16[:, :])
                last.then_inc(s_fT, 1)

            def route(g):
                pe.wait_ge(s_xT, 2 * (g + 1))
                if g >= 2:
                    pe.wait_ge(s_gcp, g - 1)
                for t in range(4):
                    for i, (a, b) in enumerate(PARTS):
                        for k in range(KH):
                            last = mm(pb[4 + g % 2][:, t * E:(t + 1) * E], xT[:, a, k, (4 * g + t) * P:(4 * g + t + 1) * P],
                                      gwp[:, b, k, :], start=(i == 0 and k == 0), stop=(i == 2 and k == 1))
                last.then_inc(s_gate, 1)

            for g in range(NG4):
                turn(g)
                if g:
                    route(g - 1)
            route(NG4 - 1)
            pe.wait_ge(s_gcp, NG4)

            def ranks():
                pe.wait_ge(s_mask, 1)
                m = mask[:, :, :].rearrange("p t e -> p (t e)")
                mm(pb[6][:, 0:NT * E], before[:, :], m, start=True, stop=True)
                mm(pb[7][:, 0:NT * E], ones16[:, :], m, start=True, stop=True).then_inc(s_rank, 1)

            def cols(w, e, k, c0, n):
                if isinstance(e, int):
                    return w[:, e, k, c0:c0 + n]
                return w[:, :, :, :].rearrange("p e k n -> p (e k n)")[:, bass.ds(e + (k * w.shape[3] + c0), n)]

            def up(i, p, e, src):
                if not (isinstance(i, int) and i < 2):
                    pe.wait_ge(s_g, i - 1)
                for w in range(2):
                    for c in range(HC):
                        n_ = 0
                        for a, b in PARTS:
                            for k in range(KH):
                                last = mm(pb[2 * p + w][:, c * P:(c + 1) * P], cols((W12h, W12l)[a], e, k, w * HID + c * P, P),
                                          src(b, k), start=(n_ == 0), stop=(n_ == 5))
                                n_ += 1
                last.then_inc(s_h12, 1)

            def down(i, p, e):
                pe.wait_ge(s_glo, i + 1)
                if not isinstance(e, int) and not (isinstance(i, int) and i < NT + 2):
                    pe.wait_ge(s_yout, i - NT - 1)
                elif not (isinstance(i, int) and i < 2):
                    pe.wait_ge(s_acc, i - 1)
                n_ = 0
                for a, b in PARTS:
                    for c in range(HC):
                        last = mm(pb[4 + p][:, 0:D], gThl[:, p, a, c, :], cols((W3h, W3l)[b], e, c, 0, D), start=(n_ == 0), stop=(n_ == 11))
                        n_ += 1
                last.then_inc(s_y, 1)

            def up_shared(i, p):
                up(i, p, E, lambda b, k: xT[:, b, k, bass.ds(i * P, P)])

            up_shared(0, 0)
            up_shared(1, 1)
            down(0, 0, E)
            ranks()
            with pe.Fori(1, NT // 2) as h:
                i = pe.snap(h * 2)
                up_shared(i, 0)
                down(pe.snap(i - 1), 1, E)
                up_shared(pe.snap(i + 1), 1)
                down(i, 0, E)
            down(NT - 1, 1, E)

            def which(h):
                digits = pe.value_load(texp[0:1, bass.ds(h, 1)], min_val=0, max_val=E ** (RING + 1) - 1)
                at = []
                for i in range(RING + 1):
                    e = pe.snap((digits // E ** i) % E)
                    at.append((pe.snap(e * (KH * 2 * HID)), pe.snap(e * (HC * D))))
                return at

            def turn_slots(j, b, nth):
                p = b % 2
                pe.wait_ge(s_xg[b], 16 * nth)
                if not (isinstance(j, int) and j < 2):
                    pe.wait_ge(s_txcp, j - 1)
                dst = pb[6 + p][:, 0:D].bitcast(f16).rearrange("p (a k n) -> p a k n", a=2, k=KH)
                for a in range(2):
                    for k in range(KH):
                        last = nc.tensor.transpose(dst[:, a, k, :], xg[b][:, a * D + k * P:a * D + (k + 1) * P], ident16[:, :])
                last.then_inc(s_tx, 1)

            def up_slots(j, p, e):
                pe.wait_ge(s_txcp, j + 1)
                up(j + NT, p, e, lambda b, k: xTg[:, p, b, k, :])

            pe.wait_ge(s_texp, 1)
            turn_slots(0, 0, 1)

            def round_(h, first=False, last=False):
                if isinstance(h, int):
                    tile = [RING * h + i for i in range(-1, RING + 1)]
                else:
                    tile = [pe.snap(h * RING + i) for i in range(-1, RING + 1)]
                at = which(h)
                prev = None if first else at.pop(0)
                at = at[-RING:]
                for i in range(RING):
                    j = tile[i + 1]
                    up_slots(j, i % 2, at[i][0])
                    if i + 1 < RING:
                        turn_slots(tile[i + 2], i + 1, h + 1)
                    elif not last:
                        turn_slots(tile[i + 2], 0, h + 2)
                    if prev:
                        down(tile[i] + NT, (i + 1) % 2, prev[1])
                    prev = at[i]
                if last:
                    down(tile[RING] + NT, (RING - 1) % 2, prev[1])

            round_(0, first=True)
            with pe.Fori(1, SLOT_TILES // RING - 1) as h:
                round_(h)
            round_(SLOT_TILES // RING - 1, last=True)

        @block.scalar
        def _(act):
            A = nc.scalar.activation

            def expert_high(e):
                act.wait_ge(s_fstage[e % 2], 48 * (e // 2 + 1))
                A(W12h[:, e, :, :].rearrange("p k n -> p (k n)"), FST[e % 2][:, 0:FW12], ACT.Copy, scale=WS)
                A(W3h[:, e, :, :].rearrange("p k n -> p (k n)"), FST[e % 2][:, FW12:], ACT.Copy, scale=WS).then_inc(s_fhi, 1)

            for e in range(EARLY):
                expert_high(e)
            n = steps(act)

            def chunk(step, v0, j):
                act.wait_ge(s_wtr[j], step + 1)
                if not (isinstance(step, int) and step == 0):
                    act.wait_ge(s_wst[j], step * 16)
                A(VR[j][:, 0:2, :].rearrange("p a b -> p (a b)"), pb[2 * j][:, :], ACT.Copy).then_inc(s_wcp[j], 1)
                act.wait_ge(s_wcp[j], (step + 1) * 2)
                act.wait_ge(s_reuse, step // STRETCH + 1)
                act.dma_start(emb_rows[bass.ds(v0, VCH), :].rearrange("(v p) d -> p v d", p=P), VR[j][:, :, :]).then_inc(s_wst[j], 16)

            for j in range(VBUF):
                chunk(0, j * VCH, j)
            with act.Fori(1, n) as step:
                for j in range(VBUF):
                    r0 = first_column(act, step, j) - (step // STRETCH) * VROWS
                    chunk(step, act.snap(r0).with_bounds(min_val=0, max_val=VROWS - VCH, guaranteed_mod_val=0, out_of_modulus=1), j)
            for e in range(EARLY, NE):
                expert_high(e)

            def cut(n, l, s):
                at = bass.ds(s * WSN, WSN)
                act.wait_ge(s_wstage, 32 * (l + 1))
                wait(act, s_wnlo, n)
                A(Wsc[:, :], Wst[:, at], ACT.Copy, scale=WS).then_inc(s_wsc, 1)
                act.wait_ge(s_wsc, n + 1)
                if not (isinstance(l, int) and l == 0):
                    act.wait_ge(s_wo, 32 * l)
                A(Wn[:, 0, at], Wsc[:, :], ACT.Copy).then_inc(s_wnhi, 1)

            for n_ in range(WSL):
                cut(n_, 0, n_)

            def one(t, prep):
                u = t + 1
                if have(t):
                    act.wait_ge(s_v, t + 1)
                    wait(act, s_o, t)
                    A(vT[:, 0, :, :], v_ps, ACT.Copy, scale=1.0 / WS).then_inc(s_vhi, 1)
                if have(t):
                    act.wait_ge(s_m, t + 1)
                    act.wait_ge(s_rzq, t + 1)
                    wait(act, s_p, t)
                    for k in range(KH):
                        last = A(MT[:, 0, k, :], m_ps[:, k, :], ACT.Copy, scale=rzq[:, k:k + 1])
                    last.then_inc(s_mhi, 1)
                if have(u):
                    act.wait_ge(s_nqmax, u + 1)
                    wait(act, s_eqlo, u)
                    wait(act, s_rzq, u)
                    for k in range(KH):
                        last = A(EQ[:, k, :], q_ps[:, k, :], ACT.Exp, bias=nqmax[:, k:k + 1], scale=1.0 / WS, accum_out=zq[:, k:k + 1])
                    last.then_inc(s_eq, 1)
                    wait(act, s_tq, u)
                    for k in range(KH):
                        last = A(EQhl[:, 0, k, :], q_ps[:, k, :], ACT.Exp, bias=nqmax[:, k:k + 1], scale=1.0 / WS)
                    last.then_inc(s_eqhi, 1)
                    act.wait_ge(s_nkmax, u + 1)
                    wait(act, s_klo, u)
                    for k in range(TB):
                        last = A(EK[:, k, :], k_ps[:, k, :], ACT.Exp, bias=nkmax[:, k:k + 1], scale=1.0 / WS, accum_out=zk[:, k:k + 1])
                    last.then_inc(s_ek, 1)
                if have(t):
                    act.wait_ge(s_p, t + 1)
                    wait(act, s_o, t)
                    A(PR[:, 0, :, :], p_ps, ACT.Copy, scale=PS / (KS * WS)).then_inc(s_phi, 1)
                if have(u):
                    act.wait_ge(s_rzks, u + 1)
                    wait(act, s_m, u)
                    for k in range(TB):
                        last = A(khl[:, 0, k, :], EK[:, k, :], ACT.Copy, scale=rzks[:, k:k + 1])
                    last.then_inc(s_khi, 1)
                if have(t + 2):
                    act.wait_ge(s_th, t + 3)
                    if have(u):
                        act.wait_ge(s_v, u + 1)
                    A(hT[:, :, :, :], hT_ps, ACT.Copy).then_inc(s_hT, 1)
                if have(u):
                    act.wait_ge(s_tq, u + 1)
                    A(eqT[:, :, :, :], eqT_ps, ACT.Copy).then_inc(s_eqT, 1)
                if prep:
                    l = layer(t) + 1
                    cut(t + WSL if isinstance(t, int) else act.snap(WSL * l + t % WSL), l, t % WSL)

            item_loop(act, one, 2, prepare=True)

            act.wait_ge(s_gw, 16)
            A(gwp[:, 0, :, :], gw[:, :, :], ACT.Copy).then_inc(s_gwhi, 1)

            def turned(g):
                act.wait_ge(s_fT, g + 1)
                for a in range(2):
                    A(xT[:, a, :, g * 4 * P:(g + 1) * 4 * P],
                      pb[2 * (g % 2) + a][:, :].bitcast(f16).rearrange("p (k n) -> p k n", k=KH), ACT.Copy).then_inc(s_xT, 1)

            for g in range(NG4):
                act.wait_ge(s_xf, g + 1)
                if g >= 2:
                    act.wait_ge(s_fT, g - 1)
                    act.wait_ge(s_xst[g % 2], 16 * (g // 2))
                A(xhl[:, g % 2, :, 0, :], xf[:, g % 2, :, :], ACT.Copy).then_inc(s_fxhi, 1)
                if g:
                    turned(g - 1)
            turned(NG4 - 1)
            act.wait_ge(s_gap, 1)
            A(gexp[:, :], gap[:, :], ACT.Exp).then_inc(s_gexp, 1)

            for w in range(2):
                act.wait_ge(s_xst[w], 16 * NG4 // 2)

            def gate(i, p, between=None):
                act.wait_ge(s_h12, i + 1)
                if not (isinstance(i, int) and i < 2):
                    act.wait_ge(s_g, i - 1)
                A(silu[:, p, :, :], pb[2 * p][:, :].rearrange("p (c n) -> p c n", c=HC), ACT.Silu, scale=1.0 / WS).then_inc(s_silu, 1)
                if between:
                    between()
                act.wait_ge(s_g, i + 1)
                if not (isinstance(i, int) and i < 2):
                    act.wait_ge(s_y, i - 1)
                A(gThl[:, p, 0, :, :], gT32[:, p, :, :], ACT.Copy).then_inc(s_ghi, 1)

            gate(0, 0)
            gate(1, 1)
            with act.Fori(1, NT // 2) as h:
                i = act.snap(h * 2)
                gate(i, 0)
                gate(act.snap(i + 1), 1)

            def turned_slots(j, p):
                act.wait_ge(s_tx, j + 1)
                A(xTg[:, p, :, :, :], pb[6 + p][:, 0:D].bitcast(f16).rearrange("p (a k n) -> p a k n", a=2, k=KH), ACT.Copy)\
                    .then_inc(s_txcp, 1)

            turned_slots(0, 0)
            with act.Fori(0, SLOT_TILES // 2 - 1) as h:
                j = act.snap(h * 2)
                gate(j + NT, 0, lambda: turned_slots(j + 1, 1))
                gate(j + NT + 1, 1, lambda: turned_slots(j + 2, 0))
            gate(SLOT_TILES - 2 + NT, 0, lambda: turned_slots(SLOT_TILES - 1, 1))
            gate(SLOT_TILES - 1 + NT, 1)

        @block.vector
        def _(dve):
            V = nc.vector
            dve.wait_ge(s_idrow, 16)
            V.tensor_reduce(idmax[:, 0:1], idrow[:, :], AX.X, ALU.max).then_inc(s_idmax, 1)
            dve.wait_ge(s_idmax, 1)

            def expert_low(e):
                dve.wait_ge(s_fstage[e % 2], 48 * (e // 2 + 1))
                dve.wait_ge(s_fhi, e + 1)
                V.scalar_tensor_tensor(W12l[:, e, :, :].rearrange("p k n -> p (k n)"), FST[e % 2][:, 0:FW12], WS,
                                       W12h[:, e, :, :].rearrange("p k n -> p (k n)"), ALU.mult, ALU.subtract)
                V.scalar_tensor_tensor(W3l[:, e, :, :].rearrange("p k n -> p (k n)"), FST[e % 2][:, FW12:], WS,
                                       W3h[:, e, :, :].rearrange("p k n -> p (k n)"), ALU.mult, ALU.subtract).then_inc(s_flo, 1)

            for e in range(EARLY):
                expert_low(e)
            n = steps(dve)

            def chunk(step, j):
                dve.wait_ge(s_wtr[j], step + 1)
                if not (isinstance(step, int) and step == 0):
                    dve.wait_ge(s_wst[j], step * 16)
                V.tensor_copy(VR[j][:, 2:4, :].rearrange("p a b -> p (a b)"), pb[2 * j + 1][:, :]).then_inc(s_wcp[j], 1)

            for j in range(VBUF):
                chunk(0, j)
            with dve.Fori(1, n) as step:
                for j in range(VBUF):
                    chunk(step, j)
            for e in range(EARLY, NE):
                expert_low(e)

            def first_stats(g):
                dve.wait_ge(s_gath[g], (n // STRETCH) * 128)
                if g:
                    dve.wait_ge(s_stat, 8 * g)
                for t in range(8 * g, 8 * g + 8):
                    V.bn_stats(stats[:, t % 8, :], X[:, t, :]).then_inc(s_st, 1)
                dve.wait_ge(s_st, 8 * (g + 1))
                for t in range(8 * g, 8 * g + 8):
                    V.bn_aggr(mv[:, t, :], stats[:, t % 8:t % 8 + 1, :]).then_inc(s_stat, 1)

            first_stats(0)
            for g in range(4):
                if g < 3:
                    first_stats(g + 1)
                dve.wait_ge(s_h0st[g], 16)
                dve.wait_ge(s_rstd, g + 1)
                for t in range(8 * g, 8 * g + 8):
                    last = V.tensor_scalar(X[:, t, :], X[:, t, :], mv[:, t, 0:1], rstd[:, t:t + 1], ALU.subtract, ALU.mult)
                    if t % TB == TB - 1:
                        last.then_inc(s_x, 1)

            def norm(u):
                dve.wait_ge(s_arstd, u + 1)
                wait(dve, s_hhi, u)
                for k in range(TB):
                    last = V.tensor_scalar(xn[:, k, :], X[:, bass.ds(seq(u) * TB + k, 1), :].rearrange("p a n -> p (a n)"),
                                           amv[:, k, 0:1], arstd[:, k:k + 1], ALU.subtract, ALU.mult)
                last.then_inc(s_xn, 1)

            def add(t):
                dve.wait_ge(s_o, t + 1)
                dve.wait_ge(s_xb, t + 1)
                V.scalar_tensor_tensor(tiles(t), o_ps, 1.0 / PS, tiles(t), ALU.mult, ALU.add).then_inc(s_x, 1)

            def one(t, prep):
                u, w = t + 1, t + 3
                if have(t - 1):
                    add(t - 1)
                if have(w):
                    dve.wait_ge(s_x, w + 1)
                    for k in range(TB):
                        V.bn_stats(stats[:, k, :], X[:, bass.ds(seq(w) * TB + k, 1), :].rearrange("p a n -> p (a n)")).then_inc(s_astat, 1)
                if have(t):
                    dve.wait_ge(s_vhi, t + 1)
                    V.scalar_tensor_tensor(vT[:, 1, :, :], v_ps, 1.0 / WS, vT[:, 0, :, :], ALU.mult, ALU.subtract).then_inc(s_vlo, 1)
                if have(u):
                    dve.wait_ge(s_q, u + 1)
                    V.tensor_reduce(qmax[:, :], q_ps, AX.X, ALU.max).then_inc(s_qmax, 1)
                    dve.wait_ge(s_qmax, u + 1)
                    wait(dve, s_eqhi, u)
                    V.tensor_scalar(nqmax[:, :], qmax[:, :], -1.0 / WS, None, ALU.mult).then_inc(s_nqmax, 1)
                if have(t):
                    dve.wait_ge(s_mhi, t + 1)
                    if have(w):
                        dve.wait_ge(s_astat, (w + 1) * TB)
                        wait(dve, s_avar, w)
                    for k in range(KH):
                        last = V.scalar_tensor_tensor(MT[:, 1, k, :], m_ps[:, k, :], rzq[:, k:k + 1], MT[:, 0, k, :], ALU.mult, ALU.subtract)
                    last.then_inc(s_mlo, 1)
                if have(w):
                    if not have(t):
                        dve.wait_ge(s_astat, (w + 1) * TB)
                        wait(dve, s_avar, w)
                    for k in range(TB):
                        last = V.bn_aggr(amv[:, k, :], stats[:, k:k + 1, :])
                    last.then_inc(s_amv, 1)
                if have(u):
                    dve.wait_ge(s_k, u + 1)
                    V.tensor_reduce(kmax[:, :], k_ps, AX.X, ALU.max).then_inc(s_kmax, 1)
                    dve.wait_ge(s_kmax, u + 1)
                    V.tensor_scalar(nkmax[:, :], kmax[:, :], -1.0 / WS, None, ALU.mult).then_inc(s_nkmax, 1)
                    dve.wait_ge(s_eqhi, u + 1)
                    V.reciprocal(rzq[:, :], zq[:, :]).then_inc(s_rzq, 1)
                    V.tensor_tensor(EQhl[:, 1, :, :], EQ[:, :, :], EQhl[:, 0, :, :], ALU.subtract).then_inc(s_eqlo, 1)
                    dve.wait_ge(s_ek, u + 1)
                    V.reciprocal(rzk[:, :], zk[:, :]).then_inc(s_rzk, 1)
                    dve.wait_ge(s_rzk, u + 1)
                    V.tensor_scalar(rzks[:, :], rzk[:, :], KS, None, ALU.mult).then_inc(s_rzks, 1)
                if have(w):
                    norm(w)
                if have(t):
                    dve.wait_ge(s_phi, t + 1)
                    V.scalar_tensor_tensor(PR[:, 1, :, :], p_ps, PS / (KS * WS), PR[:, 0, :, :], ALU.mult, ALU.subtract).then_inc(s_plo, 1)
                if have(u):
                    dve.wait_ge(s_rzks, u + 1)
                    dve.wait_ge(s_khi, u + 1)
                    for k in range(TB):
                        last = V.scalar_tensor_tensor(khl[:, 1, k, :], EK[:, k, :], rzks[:, k:k + 1], khl[:, 0, k, :], ALU.mult, ALU.subtract)
                    last.then_inc(s_klo, 1)

            item_loop(dve, one, 3)
            add(ITEMS - 1)

            dve.wait_ge(s_x, NB + ITEMS)

            def gates_out(g):
                dve.wait_ge(s_gate, g + 1)
                V.tensor_copy(gates[:, 4 * g:4 * g + 4, :], pb[4 + g % 2][:, 0:4 * E].rearrange("p (t e) -> p t e", t=4)).then_inc(s_gcp, 1)

            dve.wait_ge(s_gwhi, 1)
            V.tensor_tensor(gwp[:, 1, :, :], gw[:, :, :], gwp[:, 0, :, :], ALU.subtract).then_inc(s_gwlo, 1)

            def add_h0(g):
                x4 = X[:, 4 * g:4 * g + 4, :]
                dve.wait_ge(s_h0ld[g % 2], 16 * (g // 2 + 1))
                V.tensor_tensor(x4, x4, h0b[:, g % 2, :, :], ALU.add).then_inc(s_h1, 1)
                dve.wait_ge(s_h1, g + 1)
                half = 4 * (g % 2)
                for t in range(4):
                    V.bn_stats(stats[:, half + t, :], X[:, 4 * g + t, :]).then_inc(s_st, 1)
                dve.wait_ge(s_st, NT + 4 * (g + 1))
                for t in range(4):
                    V.bn_aggr(mv[:, 4 * g + t, :], stats[:, half + t:half + t + 1, :]).then_inc(s_stat, 1)

            add_h0(0)
            for g in range(NG4):
                if g + 1 < NG4:
                    add_h0(g + 1)
                dve.wait_ge(s_rstd, 4 + g + 1)
                if g >= 2:
                    dve.wait_ge(s_fxlo, g - 1)
                for t in range(4):
                    last = V.tensor_scalar(xf[:, g % 2, t, :], X[:, 4 * g + t, :], mv[:, 4 * g + t, 0:1], rstd[:, 4 * g + t:4 * g + t + 1],
                                           ALU.subtract, ALU.mult)
                last.then_inc(s_xf, 1)
                if g >= 2:
                    gates_out(g - 2)
            gates_out(NG4 - 2)
            gates_out(NG4 - 1)

            count = [0]

            def link(ins):
                count[0] += 1
                ins.then_inc(s_route, 1)
                dve.wait_ge(s_route, count[0])

            dve.wait_ge(s_gcp, NG4)
            for w in range(2):
                dve.wait_ge(s_xst[w], 16 * NG4 // 2)
            for t in range(NT):
                last = V.max(top8[:, t, :], gates[:, t, :])
            link(last)
            for t in range(NT):
                last = V.max_index(idx8[:, t, :], top8[:, t, :], gates[:, t, :])
            link(last)
            link(V.tensor_copy(idxf[:, :, :], idx8[:, :, :]))
            dve.wait_ge(s_ffnc, 1)
            link(V.tensor_copy(iota8f[:, :], iota8[:, :]))
            V.tensor_tensor(gap[:, :], top8[:, :, 1], top8[:, :, 0], ALU.subtract).then_inc(s_gap, 1)
            dve.wait_ge(s_gexp, 1)
            link(V.tensor_scalar(gden[:, :], gexp[:, :], 1.0, None, ALU.add))
            link(V.reciprocal(prob[:, 0, :], gden[:, :]))
            link(V.tensor_tensor(prob[:, 1, :], prob[:, 0, :], gexp[:, :], ALU.mult))
            shape = [P, NT, E]
            for c in range(TOPK):
                link(V.tensor_tensor(hot[:, c, :, :], idxf[:, :, c:c + 1].broadcast_to(shape),
                                     iota8f[:, :].unsqueeze(1).broadcast_to(shape), ALU.is_equal))
            V.tensor_tensor(mask[:, :, :], hot[:, 0, :, :], hot[:, 1, :, :], ALU.add).then_inc(s_mask, 1)
            link(V.tensor_scalar(pay[:, :, :, 1].bitcast(f32), prob[:, :, :], 1.0 / WS, None, ALU.mult))

            def gated(i, p):
                dve.wait_ge(s_silu, i + 1)
                if not (isinstance(i, int) and i < 2):
                    dve.wait_ge(s_ghi, i - 1)
                V.scalar_tensor_tensor(gT32[:, p, :, :], pb[2 * p + 1][:, :].rearrange("p (c n) -> p c n", c=HC), 1.0 / WS,
                                       silu[:, p, :, :], ALU.mult, ALU.mult).then_inc(s_g, 1)

            def glow(i, p):
                dve.wait_ge(s_ghi, i + 1)
                V.tensor_tensor(gThl[:, p, 1, :, :], gT32[:, p, :, :], gThl[:, p, 0, :, :], ALU.subtract).then_inc(s_glo, 1)

            def share(i, p):
                dve.wait_ge(s_y, i + 1)
                x = X[:, bass.ds(i, 1), :].rearrange("p a n -> p (a n)")
                V.scalar_tensor_tensor(x, pb[4 + p][:, 0:D], 1.0 / WS, x, ALU.mult, ALU.add).then_inc(s_acc, 1)

            for i in range(2):
                gated(i, i)
                glow(i, i)
            share(0, 0)

            dve.wait_ge(s_rank, 1)
            grid = lambda bank: pb[bank][:, 0:NT * E].rearrange("p (t e) -> p t e", t=NT)
            V.tensor_copy(place[:, :, :], grid(6))
            link(V.tensor_copy(totals[:, :, :], grid(7)))
            link(V.tensor_copy(scan[:, 0, :, :], totals[:, :, :]))
            src, step = 0, 1
            while step < NT:
                V.tensor_copy(scan[:, 1 - src, 0:step, :], scan[:, src, 0:step, :])
                link(V.tensor_tensor(scan[:, 1 - src, step:, :], scan[:, src, step:, :], scan[:, src, 0:NT - step, :], ALU.add))
                src, step = 1 - src, 2 * step
            link(V.tensor_copy(counti[:, 0, :], scan[:, src, NT - 1, :]))
            link(V.tensor_scalar(counti[:, 1, :], counti[:, 0, :], P - 1, None, ALU.add))
            link(V.tensor_scalar(counti[:, 2, :], counti[:, 1, :], P.bit_length() - 1, None, ALU.arith_shift_right))
            link(V.tensor_copy(ends[:, 4, :], counti[:, 2, :]))
            link(V.tensor_copy(ends[:, 0, :], ends[:, 4, :]))
            at, step = 0, 1
            while step < E:
                V.tensor_copy(ends[:, 1 - at, 0:step], ends[:, at, 0:step])
                link(V.tensor_tensor(ends[:, 1 - at, step:], ends[:, at, step:], ends[:, at, 0:E - step], ALU.add))
                at, step = 1 - at, 2 * step
            link(V.tensor_tensor(ends[:, 2, :], ends[:, at, :], ends[:, 4, :], ALU.subtract))
            link(V.tensor_scalar(ends[:, 3, :], ends[:, 2, :], float(P), None, ALU.mult))
            link(V.tensor_tensor(scan[:, 1 - src, :, :], scan[:, src, :, :], totals[:, :, :], ALU.subtract))
            link(V.tensor_tensor(place[:, :, :], place[:, :, :], scan[:, 1 - src, :, :], ALU.add))
            link(V.tensor_tensor(place[:, :, :], place[:, :, :], ends[:, 3:4, :].broadcast_to(shape), ALU.add))
            for c in range(TOPK):
                link(V.tensor_tensor(hot[:, c, :, :], hot[:, c, :, :], place[:, :, :], ALU.mult))
                link(V.tensor_reduce(slotf[:, c, :], hot[:, c, :, :], AX.X, ALU.add))
            link(V.tensor_copy(sloti[:, 0, :, :], slotf[:, :, :]))
            link(V.tensor_scalar(sloti[:, 1, :, :], sloti[:, 0, :, :], P - 1, None, ALU.bitwise_and))
            link(V.tensor_scalar(sloti[:, 2, :, :], sloti[:, 0, :, :], P.bit_length() - 1, None, ALU.arith_shift_right))
            link(V.tensor_scalar(sloti[:, 0, :, :], sloti[:, 1, :, :], SLOT_TILES, None, ALU.mult))
            V.tensor_tensor(sloti[:, 2, :, :], sloti[:, 0, :, :], sloti[:, 2, :, :], ALU.add).then_inc(s_pay, 1)
            link(V.tensor_copy(iota_tf[:, :], iota_t[:, :]))
            wide = [1, SLOT_TILES, E]
            link(V.tensor_tensor(past[:, :, :], iota_tf[:, :].unsqueeze(2).broadcast_to(wide),
                                 ends[0:1, at:at + 1, :].broadcast_to(wide), ALU.is_ge))
            link(V.tensor_reduce(texpf[:, 0, :], past[:, :, :], AX.X, ALU.add))
            link(V.tensor_scalar(texpf[:, 1, :], texpf[:, 0, :], float(E - 1), None, ALU.min))
            digit = texpf[:, 1, :].rearrange("p (h i) -> p h i", i=RING)
            top = digit[:, :, RING - 1]
            for n_, i in enumerate(range(RING - 2, -1, -1)):
                link(V.scalar_tensor_tensor(packf[:, n_ % 2, :], top, float(E), digit[:, :, i], ALU.mult, ALU.add))
                top = packf[:, n_ % 2, :]
            V.tensor_scalar(texp[:, 0:1], top[:, 0:1], float(E), None, ALU.mult)
            V.scalar_tensor_tensor(texp[:, 1:], top[:, 1:], float(E), digit[:, 0:ROUNDS - 1, RING - 1], ALU.mult, ALU.add)\
                .then_inc(s_texp, 1)

            with dve.Fori(1, NT // 2) as h:
                i = dve.snap(h * 2)
                gated(i, 0)
                share(dve.snap(i - 1), 1)
                glow(i, 0)
                j = dve.snap(i + 1)
                gated(j, 1)
                share(i, 0)
                glow(j, 1)
            share(NT - 1, 1)

            def weigh(j, p):
                dve.wait_ge(s_y, j + NT + 1)
                if not (isinstance(j, int) and j < 2):
                    dve.wait_ge(s_sadd, (j - 1) * 16)
                w = slots[:, bass.ds(j, 1), 1:2].bitcast(f32).rearrange("p a n -> p (a n)")
                V.tensor_scalar(yout[:, p, :], pb[4 + p][:, 0:D], w, None, ALU.mult).then_inc(s_yout, 1)

            def pair(j, first=False):
                gated(j + NT, 0)
                if not first:
                    weigh(j - 1, 1)
                glow(j + NT, 0)
                gated(j + NT + 1, 1)
                weigh(j, 0)
                glow(j + NT + 1, 1)

            dve.wait_ge(s_slots, 16)
            pair(0, first=True)
            with dve.Fori(1, SLOT_TILES // 2) as h:
                pair(dve.snap(h * 2))
            weigh(SLOT_TILES - 1, 1)


_INS = ["x", "L0_tok_W", "L0_attn_w_qkv", "L0_attn_w_out", "L0_attn_b_out", "L0_attn_gamma", "L0_attn_beta",
        "L0_ffn_gate_w", "L0_ffn_ew1", "L0_ffn_ew2", "L0_ffn_ew3", "L0_ffn_sw1", "L0_ffn_sw2", "L0_ffn_sw3"]


def kernel(**inputs):
    import concourse.bacc as _bacc
    from concourse.bass_utils import run_bass_kernel_spmd as _run

    nc = _bacc.Bacc("TRN2", target_bir_lowering=False, num_devices=1)
    arrays, args = {}, []
    for name in _INS:
        a = np.ascontiguousarray(inputs[name])
        arrays[f"in_{name}"] = a
        args.append(nc.dram_tensor(f"in_{name}", a.shape, mybir.dt.from_np(a.dtype), kind="ExternalInput").ap())
    shape = (*inputs["x"].shape, inputs["L0_tok_W"].shape[0])
    args.append(nc.dram_tensor("out_rows", shape, mybir.dt.float32, kind="ExternalOutput").ap())
    tower(nc, *args)
    return _run(nc, [arrays], core_ids=[0]).results[0]["out_rows"]
```
